# Optimizing a Trainium2 kernel written in Bass

```python
import numpy as np
import jax
import jax.numpy as jnp

def _softmax(x, axis=-1):
    return jax.nn.softmax(x, axis=axis)

def _gelu(x):
    return jax.nn.gelu(x, approximate=True)

def _silu(x):
    return jax.nn.silu(x)

def _sigmoid(x):
    return jax.nn.sigmoid(x)

def _layernorm(x, axis=-1, eps=1e-05):
    m = jnp.mean(x, axis=axis, keepdims=True)
    v = jnp.var(x, axis=axis, keepdims=True)
    return (x - m) / jnp.sqrt(v + eps)

def _scatter_add(tgt, idx, src, axis=0):
    return tgt.at[idx].add(src)

def _segment_sum(src, seg, n):
    return jax.ops.segment_sum(src, seg, n)
kernel_name = 'mk_prb_d1_jaxref_r8_a74348'

def setup_inputs(seed: int=0):
    np.random.seed(seed)
    _w = jnp.asarray

    def _L0_attn_setup():
        import math
        import jax, jax.numpy as jnp
        import numpy as np
        HEADS = 16
        key = jax.random.key(seed)
        k1, k2, k3, k4, k5 = jax.random.split(key, 5)
        B, S, D = (2, 256, 128)
        return {'x': jax.random.normal(k1, (B, S, D), dtype=jnp.float32), 'Wqkv': jax.random.normal(k2, (3 * D, D), dtype=jnp.float32) * (1.0 / math.sqrt(D)), 'bqkv': jax.random.normal(k3, (3 * D,), dtype=jnp.float32) * 0.02, 'Wo': jax.random.normal(k4, (D, D), dtype=jnp.float32) * (1.0 / math.sqrt(D)), 'bo': jax.random.normal(k5, (D,), dtype=jnp.float32) * 0.02}
    _L0_attn_in = _L0_attn_setup()

    def _L0_ffn_setup():
        import jax, jax.numpy as jnp
        import numpy as np
        DIM = 128
        DEPTH = 6
        HEADS = 16
        DIM_HEAD = 64
        WINDOW = 32
        INNER = HEADS * DIM_HEAD
        DIM_INNER = int(DIM * 4 * 2 / 3)
        QK_SCALE = 8.0

        def shift_tokens(t):
            a, s = jnp.split(t, 2, -1)
            s = jnp.pad(s, ((0, 0), (1, 0), (0, 0)))[:, :-1]
            return jnp.concatenate([a, s], -1)

        def l2norm(t):
            return t / jnp.maximum(jnp.linalg.norm(t, axis=-1, keepdims=True), 1e-12)

        def rotate_half(x):
            x1, x2 = jnp.split(x, 2, -1)
            return jnp.concatenate([-x2, x1], -1)

        def rotary_tables(n):
            half = jnp.arange(0, DIM_HEAD, 2, dtype=jnp.float32)
            inv_freq = 1.0 / 10000.0 ** (half / DIM_HEAD)
            t = jnp.arange(n, dtype=jnp.float32)
            freqs = t[:, None] * inv_freq[None, :]
            freqs = jnp.concatenate([freqs, freqs], -1)
            base_scale = (half + 0.4 * DIM_HEAD) / (1.4 * DIM_HEAD)
            power = (t - n // 2) / (WINDOW // 2)
            scale = base_scale[None, :] ** power[:, None]
            scale = jnp.concatenate([scale, scale], -1)
            return (freqs, scale)

        def local_attention(q, k, v):
            b, h, n, d = q.shape
            w = WINDOW
            nw = n // w
            bq = q.reshape(b, h, nw, w, d)
            bk = k.reshape(b, h, nw, w, d)
            bv = v.reshape(b, h, nw, w, d)

            def look(t):
                p = jnp.pad(t, ((0, 0), (0, 0), (1, 0), (0, 0), (0, 0)))
                return jnp.concatenate([p[:, :, :nw], p[:, :, 1:]], axis=3)
            bk2, bv2 = (look(bk), look(bv))
            seq = jnp.arange(n).reshape(nw, w)
            seq_p = jnp.pad(seq, ((1, 0), (0, 0)), constant_values=-1)
            jt = jnp.concatenate([seq_p[:nw], seq_p[1:]], axis=1)
            it = seq[:, :, None]
            jb = jt[:, None, :]
            mask = (it < jb) | (it > jb + w) | (jb == -1)
            sim = jnp.einsum('bhwie,bhwje->bhwij', bq, bk2) * QK_SCALE
            sim = jnp.where(mask, -jnp.finfo(sim.dtype).max, sim)
            attn = jax.nn.softmax(sim, -1)
            out = jnp.einsum('bhwij,bhwje->bhwie', attn, bv2)
            return out.reshape(b, h, n, d)

        def attn_layer(x, Wqkv, qs, ksc, Wo):
            b, n, _ = x.shape
            qkv = x @ Wqkv
            q, k, v = jnp.split(qkv, 3, -1)
            sh = lambda t: t.reshape(b, n, HEADS, DIM_HEAD).transpose(0, 2, 1, 3)
            q, k, v = (sh(q), sh(k), sh(v))
            q = l2norm(q) * qs
            k = l2norm(k) * ksc
            freqs, scale = rotary_tables(n)
            cos, sin = (jnp.cos(freqs), jnp.sin(freqs))
            q = q * cos * scale + rotate_half(q) * sin * scale
            inv = 1.0 / scale
            k = k * cos * inv + rotate_half(k) * sin * inv
            out = local_attention(q, k, v)
            out = out.transpose(0, 2, 1, 3).reshape(b, n, INNER)
            return out @ Wo

        def ffn_layer(x, g, bln, W1, b1, W2, b2):
            mu = x.mean(-1, keepdims=True)
            var = ((x - mu) ** 2).mean(-1, keepdims=True)
            xn = (x - mu) / jnp.sqrt(var + 1e-05) * g + bln
            hg = xn @ W1 + b1
            a, gate = jnp.split(hg, 2, -1)
            return a * jax.nn.gelu(gate, approximate=False) @ W2 + b2
        key = jax.random.key(seed)
        ks = jax.random.split(key, 8)
        B, N = (2, 256)
        init = lambda k, shape: jax.random.normal(k, shape, jnp.float32) * 0.02
        return {'x': jax.random.normal(ks[0], (B, N, DIM), jnp.float32), 'Wqkv': init(ks[1], (DEPTH, DIM, 3 * INNER)), 'q_scale': jnp.ones((DEPTH, DIM_HEAD), jnp.float32), 'k_scale': jnp.ones((DEPTH, DIM_HEAD), jnp.float32), 'Wo': init(ks[2], (DEPTH, INNER, DIM)), 'ln_g': jnp.ones((DEPTH, DIM), jnp.float32), 'ln_b': jnp.zeros((DEPTH, DIM), jnp.float32), 'W1': init(ks[3], (DEPTH, DIM, 2 * DIM_INNER)), 'b1': jnp.zeros((DEPTH, 2 * DIM_INNER), jnp.float32), 'W2': init(ks[4], (DEPTH, DIM_INNER, DIM)), 'b2': jnp.zeros((DEPTH, DIM), jnp.float32)}
    _L0_ffn_in = _L0_ffn_setup()
    _d = {'L0_attn_x': _L0_attn_in['x'], 'L0_attn_Wqkv': _L0_attn_in['Wqkv'], 'L0_attn_bqkv': _L0_attn_in['bqkv'], 'L0_attn_Wo': _L0_attn_in['Wo'], 'L0_attn_bo': _L0_attn_in['bo'], 'L0_ffn_Wqkv': _L0_ffn_in['Wqkv'], 'L0_ffn_q_scale': _L0_ffn_in['q_scale'], 'L0_ffn_k_scale': _L0_ffn_in['k_scale'], 'L0_ffn_Wo': _L0_ffn_in['Wo'], 'L0_ffn_ln_g': _L0_ffn_in['ln_g'], 'L0_ffn_ln_b': _L0_ffn_in['ln_b'], 'L0_ffn_W1': _L0_ffn_in['W1'], 'L0_ffn_b1': _L0_ffn_in['b1'], 'L0_ffn_W2': _L0_ffn_in['W2'], 'L0_ffn_b2': _L0_ffn_in['b2']}
    _x0 = _d['L0_attn_x']
    _d['L0_attn_x'] = jax.random.normal(jax.random.fold_in(jax.random.key(seed), 1), (8, 512, 128), dtype=_x0.dtype)
    del _x0
    return _d

def reference(L0_attn_x, L0_attn_Wqkv, L0_attn_bqkv, L0_attn_Wo, L0_attn_bo, L0_ffn_Wqkv, L0_ffn_q_scale, L0_ffn_k_scale, L0_ffn_Wo, L0_ffn_ln_g, L0_ffn_ln_b, L0_ffn_W1, L0_ffn_b1, L0_ffn_W2, L0_ffn_b2):

    def _L0_attn_ref(x, Wqkv, bqkv, Wo, bo):
        import math
        import jax, jax.numpy as jnp
        import numpy as np
        HEADS = 16
        B, S, D = x.shape
        H = HEADS
        hd = D // H
        qkv = x @ Wqkv.T + bqkv
        qkv = qkv.reshape(B, H, S, 3 * hd)
        q, k, v = jnp.split(qkv, 3, axis=-1)
        scores = jnp.einsum('bhsd,bhtd->bhst', q, k) * (1.0 / math.sqrt(hd))
        attn = jax.nn.softmax(scores, axis=-1)
        vals = jnp.einsum('bhst,bhtd->bhsd', attn, v)
        vals = vals.reshape(B, S, D)
        return vals @ Wo.T + bo

    def _L0_ffn_ref(x, Wqkv, q_scale, k_scale, Wo, ln_g, ln_b, W1, b1, W2, b2):
        import jax, jax.numpy as jnp
        import numpy as np
        DIM = 128
        DEPTH = 6
        HEADS = 16
        DIM_HEAD = 64
        WINDOW = 32
        INNER = HEADS * DIM_HEAD
        DIM_INNER = int(DIM * 4 * 2 / 3)
        QK_SCALE = 8.0

        def shift_tokens(t):
            a, s = jnp.split(t, 2, -1)
            s = jnp.pad(s, ((0, 0), (1, 0), (0, 0)))[:, :-1]
            return jnp.concatenate([a, s], -1)

        def l2norm(t):
            return t / jnp.maximum(jnp.linalg.norm(t, axis=-1, keepdims=True), 1e-12)

        def rotate_half(x):
            x1, x2 = jnp.split(x, 2, -1)
            return jnp.concatenate([-x2, x1], -1)

        def rotary_tables(n):
            half = jnp.arange(0, DIM_HEAD, 2, dtype=jnp.float32)
            inv_freq = 1.0 / 10000.0 ** (half / DIM_HEAD)
            t = jnp.arange(n, dtype=jnp.float32)
            freqs = t[:, None] * inv_freq[None, :]
            freqs = jnp.concatenate([freqs, freqs], -1)
            base_scale = (half + 0.4 * DIM_HEAD) / (1.4 * DIM_HEAD)
            power = (t - n // 2) / (WINDOW // 2)
            scale = base_scale[None, :] ** power[:, None]
            scale = jnp.concatenate([scale, scale], -1)
            return (freqs, scale)

        def local_attention(q, k, v):
            b, h, n, d = q.shape
            w = WINDOW
            nw = n // w
            bq = q.reshape(b, h, nw, w, d)
            bk = k.reshape(b, h, nw, w, d)
            bv = v.reshape(b, h, nw, w, d)

            def look(t):
                p = jnp.pad(t, ((0, 0), (0, 0), (1, 0), (0, 0), (0, 0)))
                return jnp.concatenate([p[:, :, :nw], p[:, :, 1:]], axis=3)
            bk2, bv2 = (look(bk), look(bv))
            seq = jnp.arange(n).reshape(nw, w)
            seq_p = jnp.pad(seq, ((1, 0), (0, 0)), constant_values=-1)
            jt = jnp.concatenate([seq_p[:nw], seq_p[1:]], axis=1)
            it = seq[:, :, None]
            jb = jt[:, None, :]
            mask = (it < jb) | (it > jb + w) | (jb == -1)
            sim = jnp.einsum('bhwie,bhwje->bhwij', bq, bk2) * QK_SCALE
            sim = jnp.where(mask, -jnp.finfo(sim.dtype).max, sim)
            attn = jax.nn.softmax(sim, -1)
            out = jnp.einsum('bhwij,bhwje->bhwie', attn, bv2)
            return out.reshape(b, h, n, d)

        def attn_layer(x, Wqkv, qs, ksc, Wo):
            b, n, _ = x.shape
            qkv = x @ Wqkv
            q, k, v = jnp.split(qkv, 3, -1)
            sh = lambda t: t.reshape(b, n, HEADS, DIM_HEAD).transpose(0, 2, 1, 3)
            q, k, v = (sh(q), sh(k), sh(v))
            q = l2norm(q) * qs
            k = l2norm(k) * ksc
            freqs, scale = rotary_tables(n)
            cos, sin = (jnp.cos(freqs), jnp.sin(freqs))
            q = q * cos * scale + rotate_half(q) * sin * scale
            inv = 1.0 / scale
            k = k * cos * inv + rotate_half(k) * sin * inv
            out = local_attention(q, k, v)
            out = out.transpose(0, 2, 1, 3).reshape(b, n, INNER)
            return out @ Wo

        def ffn_layer(x, g, bln, W1, b1, W2, b2):
            mu = x.mean(-1, keepdims=True)
            var = ((x - mu) ** 2).mean(-1, keepdims=True)
            xn = (x - mu) / jnp.sqrt(var + 1e-05) * g + bln
            hg = xn @ W1 + b1
            a, gate = jnp.split(hg, 2, -1)
            return a * jax.nn.gelu(gate, approximate=False) @ W2 + b2
        for i in range(DEPTH):
            x = attn_layer(shift_tokens(x), Wqkv[i], q_scale[i], k_scale[i], Wo[i]) + x
            x = ffn_layer(shift_tokens(x), ln_g[i], ln_b[i], W1[i], b1[i], W2[i], b2[i]) + x
        return x
    x = L0_attn_x
    xn = _layernorm(x, axis=-1)
    x = x + _L0_attn_ref(xn, L0_attn_Wqkv, L0_attn_bqkv, L0_attn_Wo, L0_attn_bo) + _L0_ffn_ref(xn, L0_ffn_Wqkv, L0_ffn_q_scale, L0_ffn_k_scale, L0_ffn_Wo, L0_ffn_ln_g, L0_ffn_ln_b, L0_ffn_W1, L0_ffn_b1, L0_ffn_W2, L0_ffn_b2)
    return x

_drawn_inputs = setup_inputs


def setup_inputs(seed=0):
    import zlib

    import numpy as np

    out = dict(_drawn_inputs(seed))
    spreads = {'L0_ffn_q_scale': (1.0, 0.6),
     'L0_ffn_k_scale': (1.0, 0.6),
     'L0_ffn_ln_g': (1.0, 0.6),
     'L0_ffn_ln_b': (0.0, 0.8),
     'L0_ffn_b1': (0.0, 0.8),
     'L0_ffn_b2': (0.0, 0.1)}
    factors = {'L0_attn_bqkv': 39.306, 'L0_attn_bo': 16.892, 'L0_ffn_W1': 3.651, 'L0_ffn_W2': 3.586}
    for name, (base, spread) in spreads.items():
        noise = np.random.default_rng([zlib.crc32(name.encode()), seed]).standard_normal(out[name].shape)
        drawn = base * np.exp(spread * noise) if base else spread * noise
        out[name] = jnp.asarray(drawn.astype(out[name].dtype))
    for name, factor in factors.items():
        out[name] = (out[name] * factor).astype(out[name].dtype)
    return out
```

```python
import numpy as np
import concourse.bass as bass
from concourse import mybir
from contextlib import ExitStack

F32 = mybir.dt.float32
BF16 = mybir.dt.bfloat16
I32 = mybir.dt.int32
ALU = mybir.AluOpType
ACT = mybir.ActivationFunctionType
AX = mybir.AxisListType

P = 128
D = 128
BATCH, SEQ = 8, 512
TOKENS = BATCH * SEQ
TILES = TOKENS // P
HEADS = 16

HD = D // HEADS
CH = SEQ // 32
HPT = P // 32
SLOTS = 64
SHIFT_ROW = 6 * HD

DEPTH, DH, WIN = 6, 64, 32
INNER = HEADS * DH
QCH = INNER // P
DIN = int(D * 4 * 2 / 3)
NJ = 3
JW = (DIN + NJ - 1) // NJ
TPB = SEQ // P
EPS = 1e-5
MASKED = -1.0e30
VA = DH + 1


def layer_norm_and_transpose(nc, io, res, xT, ident):
    with ExitStack() as ctx:
        sb = lambda n, s, d=F32: ctx.enter_context(nc.sbuf_tensor(n, s, d))
        sem = lambda n: ctx.enter_context(nc.semaphore(n))
        xn = sb("ln_xn", [P, TILES, D])
        stats = sb("ln_stats", [P, TILES, 6])
        agg = sb("ln_agg", [P, TILES, 2])
        std = sb("ln_std", [P, TILES])
        rstd = sb("ln_rstd", [P, TILES])
        bo = sb("ln_bo", [P, D])
        ps = [ctx.enter_context(nc.psum_tensor(f"ln_ps{i}", [P, 4 * P], F32)) for i in range(2)]
        loaded, stats_done, agg_done, std_done, rstd_done, xn_done, moved, transposed = map(
            sem, ("ln_loaded", "ln_stats_done", "ln_agg_done", "ln_std_done", "ln_rstd_done", "ln_xn_done",
                  "ln_moved", "ln_transposed"))
        block = ctx.enter_context(nc.Block())

        @block.sync
        def _(sp):
            sp.dma_start(res[:, :, :], io["x"].rearrange("(n p) d -> p n d", p=P)).then_inc(loaded, 16)
            sp.dma_start(ident[:, :], io["ident"]).then_inc(loaded, 16)
            sp.dma_start(bo[:, :], io["bo_rows"]).then_inc(loaded, 16)

        @block.vector
        def _(dve):
            dve.wait_ge(loaded, 48)
            for i in range(TILES):
                nc.vector.bn_stats(stats[:, i, :], res[:, i, :]).then_inc(stats_done, 1)
            for i in range(TILES):
                dve.wait_ge(stats_done, i + 1)
                nc.vector.bn_aggr(agg[:, i, :], stats[:, i, :]).then_inc(agg_done, 1)
            dve.wait_ge(agg_done, TILES)
            nc.vector.tensor_scalar(std[:, :], agg[:, :, 1], EPS, None, ALU.add).then_inc(agg_done, 1)
            dve.wait_ge(std_done, 1)
            nc.vector.reciprocal(rstd[:, :], std[:, :]).then_inc(rstd_done, 1)
            dve.wait_ge(rstd_done, 1)
            for i in range(TILES):
                nc.vector.tensor_scalar(xn[:, i, :], res[:, i, :], agg[:, i, 0:1], rstd[:, i:i + 1],
                                        ALU.subtract, ALU.mult).then_inc(xn_done, 1)
            dve.wait_ge(xn_done, TILES)
            nc.vector.tensor_tensor(res[:, :, :], res[:, :, :],
                                    bo[:, None, :].broadcast_to([P, TILES, D]), ALU.add).then_inc(xn_done, 1)

        @block.scalar
        def _(act):
            act.wait_ge(agg_done, TILES + 1)
            nc.scalar.activation(std[:, :], std[:, :], ACT.Sqrt).then_inc(std_done, 1)
            for b in range(BATCH):
                act.wait_ge(transposed, b + 1)
                nc.scalar.copy(xT[:, b, :], ps[b % 2][:, :]).then_inc(moved, 1)

        @block.tensor
        def _(pe):
            for b in range(BATCH):
                pe.wait_ge(xn_done, TPB * (b + 1))
                if b >= 2:
                    pe.wait_ge(moved, b - 1)
                for t in range(TPB):
                    last = nc.tensor.transpose(ps[b % 2][:, t * P:(t + 1) * P], xn[:, TPB * b + t, :], ident[:, :])
                last.then_inc(transposed, 1)


def global_attention(nc, io, res, xT, ident):
    with ExitStack() as ctx:
        sb = lambda n, s, d=F32: ctx.enter_context(nc.sbuf_tensor(n, s, d))
        sem = lambda n: ctx.enter_context(nc.semaphore(n))
        w_qkv = sb("at_wqkv", [P, 3 * P])
        w_o = sb("at_wo", [P, P])
        bias = sb("at_bias", [P, 3 * P])
        ident16 = sb("at_ident16", [P, P], BF16)
        xg = sb("at_xg", [P, P])
        qkv = sb("at_qkv", [P, 3, CH, HD])
        part = sb("at_part", [P, 3, 2, CH, HD], BF16)
        rest = sb("at_rest", [P, 2, CH, HD])
        stack = sb("at_stack", [P, 2, CH, SLOTS], BF16)
        qs = [sb(f"at_qs{i}", [P, HPT, CH, 32], BF16) for i in range(2)]
        ks = [sb(f"at_ks{i}", [P, HPT, CH, 32], BF16) for i in range(2)]
        vs = [sb(f"at_vs{i}", [P, HPT, 4, 32]) for i in range(2)]
        rowmax = sb("at_rowmax", [P, HPT * 4])
        mrest = sb("at_mrest", [P, HPT * 4])
        mpart = sb("at_mpart", [P, 3, HPT * 4], BF16)
        mT = sb("at_mT", [3 * HPT * 4, P], BF16)
        probs = [sb(f"at_probs{i}", [P, 2, SEQ]) for i in range(2)]
        oT = sb("at_oT", [P, CH, 32])
        rden = sb("at_rden", [P, CH])
        vals = sb("at_vals", [P, CH, HD])
        valsT = sb("at_valsT", [P, P])
        ps_exp = [ctx.enter_context(nc.psum_tensor(f"at_pe{i}", [P, 2, SEQ], F32)) for i in range(2)]
        ps_max = [ctx.enter_context(nc.psum_tensor(f"at_pm{i}", [P, SEQ], F32)) for i in range(2)]
        ps_o = ctx.enter_context(nc.psum_tensor("at_po", [P, SEQ], F32))
        ps_x = ctx.enter_context(nc.psum_tensor("at_px", [P, SEQ], F32))
        names = ("loaded", "cleared", "ident_done", "x_taken", "projected", "biased", "parted", "v_placed", "stacked",
                 "stack_transposed", "stack_moved", "scored_max", "max_done", "mpart_done", "m_transposed", "m_moved",
                 "shift_rows", "scored_exp", "exp_done", "pv_done", "o_taken", "rden_done", "vals_done", "vals_transposed",
                 "vals_moved", "y_done", "res_done", "link", "passed", "kept")
        S = {n: sem("at_" + n) for n in names}
        block = ctx.enter_context(nc.Block())
        SCALE = 1.0 / float(np.sqrt(HD))

        def passed(eng):
            eng.sem_inc(S["passed"], 1)

        def groups(eng, front, back):
            front(0, 0, None, None)
            with eng.Fori(0, TILES // 2 - 1) as i:
                front(2 * i + 1, 1, 2 * i, 0)
                front(2 * i + 2, 0, 2 * i + 1, 1)
            front(TILES - 1, 1, TILES - 2, 0)
            back(TILES - 1, 1)

        @block.sync
        def _(sp):
            sp.dma_start(w_qkv[:, :], io["at_wqkvT"]).then_inc(S["loaded"], 16)
            sp.dma_start(w_o[:, :], io["at_woT"]).then_inc(S["loaded"], 16)
            sp.dma_start(bias[:, :], io["at_bias"]).then_inc(S["loaded"], 16)

            def shift(g, par):
                sp.wait_ge(S["m_moved"], g + 1)
                sp.dma_start(qs[par][SHIFT_ROW:SHIFT_ROW + 3, :, :, :].rearrange("p h c t -> p (h c t)")
                             .rearrange("p (r q) -> p r q", q=P),
                             mT[:, :]).then_inc(S["shift_rows"], 16)
                sp.wait_ge(S["shift_rows"], 16 * g + 16)
                passed(sp)
            with sp.Fori(0, TILES // 2) as i:
                shift(2 * i, 0)
                shift(2 * i + 1, 1)
            sp.wait_ge(S["res_done"], TILES)
            sp.dma_start(io["kept"].rearrange("(n p) d -> p n d", p=P), res[:, :, :]).then_inc(S["kept"], 16)
            sp.wait_ge(S["kept"], 16)

        @block.gpsimd
        def _(pool):
            pool.memset(stack[:, :, :, :], 0.0).then_inc(S["cleared"], 1)
            pool.wait_ge(S["cleared"], 1)
            pool.memset(stack[:, 1, :, SHIFT_ROW:SHIFT_ROW + 3], 1.0).then_inc(S["cleared"], 1)
            pool.memset(ks[0][:, :, :, :], 0.0).then_inc(S["cleared"], 1)
            pool.memset(ks[1][:, :, :, :], 0.0).then_inc(S["cleared"], 1)
            pool.memset(qs[0][:, :, :, :], 0.0).then_inc(S["cleared"], 1)
            pool.memset(qs[1][:, :, :, :], 0.0).then_inc(S["cleared"], 1)
            for v in vs:
                pool.memset(v[:, :, :, :], 0.0).then_inc(S["cleared"], 1)
            pool.wait_ge(S["cleared"], 8)
            for v in vs:
                pool.memset(v[:, :, :, HD:HD + 1], 1.0).then_inc(S["cleared"], 1)
            pool.wait_ge(S["cleared"], 10)

            def place(g, *_):
                pool.wait_ge(S["parted"], g + 1)
                pool.wait_ge(S["stack_transposed"], 4 * g)
                passed(pool)
                for side, slot, p in ((0, 0, 0), (0, 1, 0), (0, 2, 1), (0, 3, 0), (0, 4, 1), (0, 5, 2),
                                      (1, 0, 0), (1, 1, 1), (1, 2, 0), (1, 3, 2), (1, 4, 1), (1, 5, 0)):
                    last = nc.gpsimd.tensor_scalar(stack[:, side, :, slot * HD:(slot + 1) * HD],
                                                   part[:, p, side, :, :], 1.0, 0.0, ALU.mult, ALU.add)
                last.then_inc(S["stacked"], 1)
            with pool.Fori(0, TILES) as g:
                place(g)

        @block.vector
        def _(dve):
            dve.wait_ge(S["loaded"], 48)
            nc.vector.tensor_copy(ident16[:, :], ident[:, :]).then_inc(S["ident_done"], 1)
            dve.wait_ge(S["cleared"], 10)
            LINKS = 9

            def front(g, par, gb, parb):
                links = [0]

                def link(ins):
                    links[0] += 1
                    ins.then_inc(S["link"], 1)
                    dve.wait_ge(S["link"], g * LINKS + links[0])
                dve.wait_ge(S["projected"], g + 1)
                nc.vector.tensor_tensor(qkv[:, :, :, :].rearrange("p a c d -> p (a c d)"), ps_x[:, 0:3 * P],
                                        bias[:, :], ALU.add).then_inc(S["biased"], 1)
                dve.wait_ge(S["biased"], g + 1)
                dve.wait_ge(S["stacked"], g)
                link(nc.vector.tensor_copy(part[:, 0], qkv[:, 0:2]))
                link(nc.vector.tensor_tensor(rest[:, :], qkv[:, 0:2], part[:, 0], ALU.subtract))
                link(nc.vector.tensor_copy(part[:, 1], rest[:, :]))
                nc.vector.tensor_tensor(part[:, 2], rest[:, :], part[:, 1], ALU.subtract).then_inc(S["parted"], 1)
                if gb is not None:
                    dve.wait_ge(S["pv_done"], 4 * gb)
                for h in range(HPT):
                    for c4 in range(4):
                        last = nc.vector.tensor_copy(
                            vs[par][32 * c4:32 * c4 + 32, h, :, 0:HD],
                            qkv[32 * h:32 * h + 32, 2, :, :].rearrange("p (b c) d -> p b c d", c=4)[:, :, c4, :])
                last.then_inc(S["v_placed"], 1)
                for h in range(HPT):
                    for qc in range(4):
                        k = 4 * h + qc
                        dve.wait_ge(S["scored_max"], 16 * g + k + 1)
                        nc.vector.reduce_max(rowmax[:, k:k + 1], ps_max[k % 2][:, :], AX.X).then_inc(S["max_done"], 1)
                dve.wait_ge(S["max_done"], 16 * g + 16)
                dve.wait_ge(S["m_transposed"], g)
                link(nc.vector.tensor_scalar(mrest[:, :], rowmax[:, :], -1.0, None, ALU.mult))
                link(nc.vector.tensor_copy(mpart[:, 0, :], mrest[:, :]))
                link(nc.vector.tensor_tensor(mrest[:, :], mrest[:, :], mpart[:, 0, :], ALU.subtract))
                link(nc.vector.tensor_copy(mpart[:, 1, :], mrest[:, :]))
                link(nc.vector.tensor_tensor(mrest[:, :], mrest[:, :], mpart[:, 1, :], ALU.subtract))
                link(nc.vector.tensor_copy(mpart[:, 2, :], mrest[:, :]))
                assert links[0] == LINKS, links
                if gb is not None:
                    back(gb, parb)

            def back(g, par):
                dve.wait_ge(S["pv_done"], 4 * g + 4)
                nc.vector.transpose(oT[:, :, :].rearrange("p c d -> p (c d)"), ps_o[:, :]).then_inc(S["o_taken"], 1)
                dve.wait_ge(S["o_taken"], g + 1)
                nc.vector.reciprocal(rden[:, :], oT[:, :, HD]).then_inc(S["rden_done"], 1)
                dve.wait_ge(S["rden_done"], g + 1)
                nc.vector.tensor_tensor(vals[:, :, :], oT[:, :, 0:HD], rden[:, :, None].broadcast_to([P, CH, HD]),
                                        ALU.mult).then_inc(S["vals_done"], 1)
                dve.wait_ge(S["y_done"], g + 1)
                nc.vector.tensor_tensor(res[:, g, :], res[:, g, :], ps_x[:, 0:P], ALU.add).then_inc(S["res_done"], 1)
            groups(dve, front, back)

        @block.scalar
        def _(act):
            act.wait_ge(S["cleared"], 10)

            def exps(g, h, par):
                for pair in range(2):
                    k = 2 * h + pair
                    act.wait_ge(S["scored_exp"], 8 * g + k + 1)
                    act.wait_ge(S["pv_done"], 4 * g + h)
                    nc.scalar.activation(probs[pair][:, :, :], ps_exp[pair][:, :, :], ACT.Exp,
                                         scale=SCALE).then_inc(S["exp_done"], 1)

            def finish(g):
                act.wait_ge(S["vals_transposed"], g + 1)
                nc.scalar.copy(valsT[:, :], ps_x[:, 0:P]).then_inc(S["vals_moved"], 1)

            def front(g, par, gb, parb):
                act.wait_ge(S["projected"], g)
                nc.scalar.copy(xg[:, :], xT[:, :, :].rearrange("p b s -> p (b s)")[:, bass.ts(g, P)]).then_inc(S["x_taken"], 1)
                for j in range(4):
                    side, half = j // 2, j % 2
                    act.wait_ge(S["stack_transposed"], 4 * g + j + 1)
                    dst = (qs, ks)[side][par][0:SLOTS, :, half * 8:half * 8 + 8, :].rearrange("p h c t -> p c h t")
                    src = ps_max[j % 2][:, :].bitcast(BF16)[0:SLOTS, :].rearrange("p (c h t) -> p c h t", h=HPT, t=32)
                    nc.scalar.copy(dst, src).then_inc(S["stack_moved"], 1)
                if gb is not None:
                    for h in range(HPT):
                        exps(gb, h, parb)
                act.wait_ge(S["shift_rows"], 16 * g)
                act.wait_ge(S["m_transposed"], g + 1)
                nc.scalar.copy(mT[:, :], ps_x[:, 0:P // 2].bitcast(BF16)[0:3 * HPT * 4, :]).then_inc(S["m_moved"], 1)
                if gb is not None:
                    finish(gb)

            def back(g, par):
                for h in range(HPT):
                    exps(g, h, par)
                finish(g)
            groups(act, front, back)

        @block.tensor
        def _(pe):
            pe.wait_ge(S["ident_done"], 1)
            pe.wait_ge(S["cleared"], 10)

            def exp_head(g, h, par):
                for pair in range(2):
                    k = 2 * h + pair
                    pe.wait_ge(S["exp_done"], 8 * g + k - 1 if h else 8 * g)
                    for i in range(2):
                        kc = 2 * pair + i
                        last = nc.tensor.matmul(
                            ps_exp[pair][:, i, :],
                            ks[par][:, h, :, :].rearrange("p c t -> p (c t)")[:, kc * P:(kc + 1) * P],
                            qs[par][:, h, :, :].rearrange("p c t -> p (c t)"), start=True, stop=True)
                    last.then_inc(S["scored_exp"], 1)
                if h == 0:
                    pe.wait_ge(S["v_placed"], g + 1)
                    pe.wait_ge(S["o_taken"], g)
                for pair in range(2):
                    pe.wait_ge(S["exp_done"], 8 * g + 2 * h + pair + 1)
                    for i in range(2):
                        kc = 2 * pair + i
                        last = nc.tensor.matmul(ps_o[32 * h:32 * h + 32, :], vs[par][:, h, kc, :], probs[pair][:, i, :],
                                                start=kc == 0, stop=kc == 3)
                last.then_inc(S["pv_done"], 1)

            def max_head(g, h, par):
                for qc in range(4):
                    k = 4 * h + qc
                    if k < 2:
                        pe.wait_ge(S["stack_moved"], 4 * g + 4)
                    else:
                        pe.wait_ge(S["max_done"], 16 * g + k - 1)
                    nc.tensor.matmul(ps_max[k % 2][:, :],
                                     qs[par][:, h, :, :].rearrange("p c t -> p (c t)")[:, qc * P:(qc + 1) * P],
                                     ks[par][:, h, :, :].rearrange("p c t -> p (c t)"),
                                     start=True, stop=True).then_inc(S["scored_max"], 1)

            def finish(g):
                pe.wait_ge(S["vals_done"], g + 1)
                nc.tensor.transpose(ps_x[:, 0:P], vals[:, :, :].rearrange("p c d -> p (c d)"), ident[:, :]).then_inc(S["vals_transposed"], 1)
                pe.wait_ge(S["vals_moved"], g + 1)
                nc.tensor.matmul(ps_x[:, 0:P], valsT[:, :], w_o[:, :], start=True, stop=True).then_inc(S["y_done"], 1)

            def front(g, par, gb, parb):
                pe.wait_ge(S["x_taken"], g + 1)
                if gb is not None:
                    pe.wait_ge(S["res_done"], gb)
                    pe.wait_ge(S["m_moved"], g)
                nc.tensor.matmul(ps_x[:, 0:3 * P], xg[:, :], w_qkv[:, :], start=True, stop=True).then_inc(S["projected"], 1)
                pe.wait_ge(S["stacked"], g + 1)
                for j in range(4):
                    side, half = j // 2, j % 2
                    if j < 2:
                        pe.wait_ge(S["max_done"], 16 * g)
                    else:
                        pe.wait_ge(S["stack_moved"], 4 * g + j - 1)
                    passed(pe)
                    for c in range(8):
                        last = nc.tensor.transpose(ps_max[j % 2][:, :].bitcast(BF16)[0:SLOTS, c * P:(c + 1) * P],
                                                   stack[:, side, 8 * half + c, :], ident16[:, :])
                    last.then_inc(S["stack_transposed"], 1)
                if gb is not None:
                    pe.wait_ge(S["shift_rows"], 16 * gb + 16)
                for h in range(HPT):
                    max_head(g, h, par)
                    if gb is not None:
                        exp_head(gb, h, parb)
                pe.wait_ge(S["biased"], g + 1)
                pe.wait_ge(S["link"], g * 9 + 9)
                passed(pe)
                nc.tensor.transpose(ps_x[:, 0:P // 2].bitcast(BF16)[0:3 * HPT * 4, :],
                                    mpart[:, :, :].rearrange("p a b -> p (a b)"), ident16[:, :]).then_inc(S["m_transposed"], 1)
                if gb is not None:
                    pe.wait_ge(S["m_moved"], g + 1)
                    finish(gb)

            def back(g, par):
                pe.wait_ge(S["shift_rows"], 16 * g + 16)
                for h in range(HPT):
                    exp_head(g, h, par)
                pe.wait_ge(S["res_done"], g)
                finish(g)
            groups(pe, front, back)


ORDER = ["P0", "P1", "T0", "S0", "P2", "T1", "R0", "V0", "S1", "P3", "T2", "O0", "R1", "V1", "S2", "T3",
         "O1", "R2", "V2", "S3", "O2", "R3", "V3", "O3", "C"]
FILLS = {"P": [("q", "dve"), ("k", "dve"), ("v", "act")],
         "T": [("qT", "act"), ("kT", "act")],
         "S": [("s", "dve")],
         "R": [("r", "act")],
         "V": [("va", "dve"), ("vb", "dve")],
         "O": [("o", "act")],
         "C": [("wo", "dve"), ("mean", "dve"), ("var", "act"), ("f0", "dve"), ("f1", "dve"), ("f2", "dve"),
               ("y", "dve")]}
FILL, READ, READS = {}, {}, {"dve": 0, "act": 0}
for _stage in ORDER:
    for _what, _engine in FILLS[_stage[0]]:
        FILL[_what + _stage[1:]] = len(FILL)
        READ[_what + _stage[1:]] = (_engine, READS[_engine])
        READS[_engine] += 1
NFILL = len(FILL)
BY_FILL = {n: k for k, n in FILL.items()}
SLOTS_PS = 4


def windowed_stack(nc, io, xT, ident):
    with ExitStack() as ctx:
        sb = lambda n, s, d=F32: ctx.enter_context(nc.sbuf_tensor(n, s, d))
        sem = lambda n: ctx.enter_context(nc.semaphore(n))
        w_qkv = sb("w_qkv", [P, 3, INNER])
        w_o = sb("w_o", [P, QCH, D])
        w_1 = sb("w_1", [P, 2, NJ, JW])
        w_2 = sb("w_2", [JW, NJ, D])
        b_1 = sb("b_1", [JW, 2, NJ])
        vec = sb("vec", [P, 3])
        qks = sb("qks", [P, 2, DH])
        rot = sb("rot", [P, TPB, 4, DH])
        table = sb("table", [P, TPB, 4, DH])
        ident16 = sb("ident16", [P, P], BF16)
        mask = sb("mask", [P, 2, SEQ], BF16)
        ones = sb("ones", [P, P])
        epsc = sb("epsc", [P, 1])
        xs = sb("xs", [P, SEQ])
        sq = sb("sq", [P, 2, HEADS, DH])
        qk = sb("qk", [P, 2, HEADS, DH])
        mask32 = sq[:, 0].rearrange("p h d -> p (h d)").rearrange("p (a n) -> p a n", a=2)
        cosq = sb("cosq", [P, 2, HEADS, 2, DH // 2])
        sinq = sb("sinq", [P, 2, HEADS, 2, DH // 2])
        ss = sb("ss", [P, 2 * HEADS])
        ry = sb("ry", [P, 2 * HEADS])
        rt = sb("rt", [P, 2 * HEADS])
        qT = sb("qT", [P, QCH, SEQ])
        kT = sb("kT", [P, QCH, WIN + SEQ])
        va = sb("va", [P, TPB, HEADS, VA])
        vb = sb("vb", [P, TPB, HEADS, VA])
        prob = sb("prob", [P, HEADS, DH])
        probT = sb("probT", [P, 8, P])
        smax = sb("smax", [P, HEADS])
        rden = sb("rden", [P, HEADS])
        o = sb("o", [P, HEADS, DH])
        oT = sb("oT", [P, QCH, SEQ])
        x1 = sb("x1", [P, SEQ])
        xs2 = sb("xs2", [P, SEQ])
        xc = sb("xc", [P, SEQ])
        sqc = sb("sqc", [P, SEQ])
        z = sb("z", [P, SEQ])
        gate = sb("gate", [JW, SEQ])
        hid = sb("hid", [JW, NJ, SEQ])
        ring = [ctx.enter_context(nc.psum_tensor(f"ring{i}", [P, 2, SEQ], F32)) for i in range(SLOTS_PS)]
        S = {n: sem("ws_" + n) for n in (
            "const_loaded", "const_ready", "weights", "tables", "filled", "dve_read", "act_read", "xs_ready",
            "squares", "sumsq", "turned", "added", "normed", "shifted", "probs", "xs2_ready", "centered_sq",
            "gates", "x_final", "link", "passed")}
        vb_ready = [sem(f"ws_vb_ready{t}") for t in range(TPB)]
        block = ctx.enter_context(nc.Block())
        NW = 7

        def passed(eng):
            eng.sem_inc(S["passed"], 1)

        def slot(what):
            return ring[FILL[what] % SLOTS_PS]

        def units(eng, layer_start, body):
            with eng.Fori(0, DEPTH) as l:
                layer_start(l)
                with eng.Fori(0, BATCH) as b:
                    body(l * BATCH + b, l, b)

        def filled(eng, it, what):
            eng.wait_ge(S["filled"], it * NFILL + FILL[what] + 1)

        def was_read(eng, it, what):
            who, n = READ[what]
            eng.wait_ge(S[who + "_read"], it * READS[who] + n + 1)

        @block.sync
        def _(sp):
            sp.dma_start(rot[:, :, :, :], io["rot"]).then_inc(S["const_loaded"], 16)
            sp.dma_start(mask32, io["mask"]).then_inc(S["const_loaded"], 16)

            def layer_start(l):
                sp.wait_ge(S["x_final"], l * BATCH)
                sp.dma_start(w_qkv[:, :, :].rearrange("p a n -> p (a n)"), io["w_qkv"][l]).then_inc(S["weights"], 16)
                sp.dma_start(qks[:, :, :].rearrange("p a n -> p (a n)"), io["qk_scale"][l]).then_inc(S["weights"], 16)
                sp.dma_start(w_o[:, :, :], io["w_o"][l].rearrange("(c p) n -> p c n", p=P)).then_inc(S["weights"], 16)
                sp.dma_start(w_1[:, :, :, :].rearrange("p a j n -> p (a j n)"), io["w_1"][l]).then_inc(S["weights"], 16)
                sp.dma_start(w_2[:, :, :], io["w_2"][l].rearrange("(j p) n -> p j n", p=JW)).then_inc(S["weights"], 16)
                sp.dma_start(b_1[:, :, :].rearrange("p a j -> p (a j)"), io["b_1"][l]).then_inc(S["weights"], 16)
                sp.dma_start(vec[:, :], io["vec"][l]).then_inc(S["weights"], 16)

            def body(it, l, b):
                for t in range(TPB):
                    was_read(sp, it, f"v{t}")
                    sp.dma_start(vb[WIN:P, t, :, :], va[0:P - WIN, t, :, :]).then_inc(vb_ready[t], 16)
                    if t:
                        sp.dma_start(vb[0:WIN, t, :, :], va[P - WIN:P, t - 1, :, :]).then_inc(vb_ready[t], 16)
            units(sp, layer_start, body)

        @block.gpsimd
        def _(pool):
            pool.memset(va[:, :, :, :], 1.0).then_inc(S["const_ready"], 1)
            pool.memset(vb[0:WIN, 0, :, :], 0.0).then_inc(S["const_ready"], 1)
            pool.memset(kT[:, :, 0:WIN], 0.0).then_inc(S["const_ready"], 1)
            pool.memset(ones[:, :], 1.0 / D).then_inc(S["const_ready"], 1)
            pool.memset(xs[:, :], 0.0).then_inc(S["const_ready"], 1)
            pool.memset(xs2[:, :], 0.0).then_inc(S["const_ready"], 1)
            pool.memset(epsc[:, :], EPS).then_inc(S["const_ready"], 1)
            pool.wait_ge(S["const_ready"], 9)

            def body(it, l, b):
                for t in range(TPB):
                    for side in range(2):
                        pool.wait_ge(S["turned"], it * 8 + 2 * t + side + 1)
                        nc.gpsimd.tensor_tensor(cosq[:, side], cosq[:, side], sinq[:, side], ALU.add).then_inc(S["added"], 1)
            units(pool, lambda l: None, body)

        @block.vector
        def _(dve):
            dve.wait_ge(S["const_loaded"], 32)
            nc.vector.tensor_copy(mask[:, :, :], mask32).then_inc(S["const_ready"], 1)
            nc.vector.tensor_copy(ident16[:, :], ident[:, :]).then_inc(S["const_ready"], 1)
            dve.wait_ge(S["const_ready"], 9)
            PER_TILE = 15
            LINKS = TPB * (PER_TILE + 1 + 2) + 3
            H = DH // 2

            def layer_start(l):
                dve.wait_ge(S["weights"], 16 * NW * (l + 1))
                for side in range(2):
                    s = qks[:, side, :]
                    nc.vector.tensor_tensor(table[:, :, 2 * side, :], rot[:, :, 2 * side, :],
                                            s[:, None, :].broadcast_to([P, TPB, DH]), ALU.mult)
                    for half in range(2):
                        other = s[:, (1 - half) * H:(2 - half) * H]
                        last = nc.vector.tensor_tensor(
                            table[:, :, 2 * side + 1, half * H:half * H + H], rot[:, :, 2 * side + 1, half * H:half * H + H],
                            other[:, None, :].broadcast_to([P, TPB, H]), ALU.mult)
                last.then_inc(S["tables"], 1)
                dve.wait_ge(S["tables"], l + 1)
                passed(dve)

            def body(it, l, b):
                links = [0]

                def link(ins):
                    links[0] += 1
                    ins.then_inc(S["link"], 1)
                    dve.wait_ge(S["link"], it * LINKS + links[0])

                def project(t):
                    for side in range(2):
                        ps = slot("qk"[side] + str(t))[:, :, :].rearrange("p a n -> p (a n)").rearrange(
                            "p (h a d) -> p h a d", h=HEADS, a=2)
                        cos, sin = table[:, t, 2 * side, :], table[:, t, 2 * side + 1, :]
                        dve.wait_ge(S["squares"], it * 8 + 2 * t + side + 1)
                        dve.wait_ge(S["normed"], it * 8 + 2 * t)
                        nc.vector.tensor_tensor(cosq[:, side].rearrange("p h a d -> p h (a d)"),
                                                ps.rearrange("p h a d -> p h (a d)"),
                                                cos[:, None, :].broadcast_to([P, HEADS, DH]), ALU.mult)
                        for half in range(2):
                            last = nc.vector.tensor_tensor(
                                sinq[:, side, :, half, :], ps[:, :, 1 - half, :],
                                sin[:, None, half * H:half * H + H].broadcast_to([P, HEADS, H]), ALU.mult)
                        last.then_inc(S["dve_read"], 1)
                        was_read(dve, it, "qk"[side] + str(t))
                        dve.sem_inc(S["turned"], 1)
                    nc.vector.reduce_sum(ss[:, :], sq[:, :, :, :].rearrange("p a h d -> p (a h) d"), AX.X).then_inc(S["sumsq"], 1)
                    dve.wait_ge(S["sumsq"], it * TPB + t + 1)
                    link(nc.vector.tensor_scalar(ss[:, :], ss[:, :], 1e-24, None, ALU.max))
                    link(nc.vector.tensor_single_scalar(rt[:, :].bitcast(I32), ss[:, :].bitcast(I32), 1, ALU.logical_shift_right))
                    link(nc.vector.tensor_scalar(ry[:, :].bitcast(I32), rt[:, :].bitcast(I32), -1.0, float(0x5F3759DF), ALU.mult, ALU.add))
                    for _ in range(3):
                        link(nc.vector.tensor_tensor(rt[:, :], ry[:, :], ss[:, :], ALU.mult))
                        link(nc.vector.tensor_tensor(rt[:, :], rt[:, :], ry[:, :], ALU.mult))
                        link(nc.vector.tensor_scalar(rt[:, :], rt[:, :], -0.5, 1.5, ALU.mult, ALU.add))
                        link(nc.vector.tensor_tensor(ry[:, :], ry[:, :], rt[:, :], ALU.mult))
                    for side in range(2):
                        dve.wait_ge(S["added"], it * 8 + 2 * t + side + 1)
                        v = cosq[:, side].rearrange("p h a d -> p h (a d)")
                        if side == 0 and t:
                            filled(dve, it, f"kT{t - 1}")
                        nc.vector.tensor_tensor(qk[:, side], v, ry[:, side * HEADS:(side + 1) * HEADS, None]
                                                .broadcast_to([P, HEADS, DH]), ALU.mult).then_inc(S["normed"], 1)

                def scores(t):
                    filled(dve, it, f"s{t}")
                    ps = slot(f"s{t}")[:, :, :].rearrange("p a n -> p (a n)").rearrange("p (s k) -> p s k", k=DH)
                    link(nc.vector.reduce_max(smax[:, :], ps, AX.X))
                    if t:
                        filled(dve, it, f"r{t - 1}")
                    nc.vector.tensor_tensor(prob[:, :, :], ps, smax[:, :, None].broadcast_to([P, HEADS, DH]),
                                            ALU.subtract).then_inc(S["dve_read"], 1)

                def outputs(t):
                    for k, name in enumerate((f"va{t}", f"vb{t}")):
                        filled(dve, it, name)
                        ps = slot(name)[:, :, 0:4 * VA].rearrange("p a (g d) -> p a g d", d=VA)
                        r = rden[:, 8 * k:8 * k + 8].rearrange("p (a g) -> p a g", a=2)
                        link(nc.vector.reciprocal(r, ps[:, :, :, DH]))
                        nc.vector.tensor_tensor(o[:, 8 * k:8 * k + 8, :].rearrange("p (a g) d -> p a g d", a=2),
                                                ps[:, :, :, 0:DH], r[:, :, :, None].broadcast_to([P, 2, 4, DH]),
                                                ALU.mult).then_inc(S["dve_read"], 1)

                def feed_forward():
                    filled(dve, it, "wo")
                    nc.vector.tensor_tensor(x1[:, :], slot("wo")[:, 0, :], xT[:, b, :], ALU.add).then_inc(S["dve_read"], 1)
                    dve.wait_ge(S["xs2_ready"], it + 1)
                    filled(dve, it, "mean")
                    nc.vector.tensor_tensor(xc[:, :], xs2[:, :], slot("mean")[:, 0, :], ALU.subtract).then_inc(S["dve_read"], 1)
                    was_read(dve, it, "var")
                    link(nc.vector.reciprocal(sqc[:, :], sqc[:, :]))
                    link(nc.vector.tensor_tensor(z[:, :], xc[:, :], sqc[:, :], ALU.mult))
                    link(nc.vector.tensor_scalar(z[:, :], z[:, :], vec[:, 0:1], vec[:, 1:2], ALU.mult, ALU.add))
                    for j in range(NJ):
                        dve.wait_ge(S["gates"], it * NJ + j + 1)
                        nc.vector.scalar_tensor_tensor(out=hid[:, j, :], in0=slot(f"f{j}")[0:JW, 0, :],
                                                       scalar=b_1[:, 0, j:j + 1], in1=gate[:, :], op0=ALU.add,
                                                       op1=ALU.mult).then_inc(S["dve_read"], 1)
                    filled(dve, it, "y")
                    nc.vector.scalar_tensor_tensor(out=xT[:, b, :], in0=slot("y")[:, 0, :], scalar=vec[:, 2:3],
                                                   in1=x1[:, :], op0=ALU.add, op1=ALU.add).then_inc(S["dve_read"], 1)
                    was_read(dve, it, "y")
                    dve.sem_inc(S["x_final"], 1)

                for stage in ORDER:
                    if stage[0] == "P":
                        project(int(stage[1]))
                    elif stage[0] == "S":
                        scores(int(stage[1]))
                    elif stage[0] == "V":
                        outputs(int(stage[1]))
                    elif stage[0] == "C":
                        feed_forward()
                assert links[0] == LINKS, (links, LINKS)
            units(dve, layer_start, body)

        @block.scalar
        def _(act):
            act.wait_ge(S["const_ready"], 9)

            def layer_start(l):
                act.wait_ge(S["x_final"], l * BATCH)
                act.wait_ge(S["tables"], l + 1)

            def body(it, l, b):
                def shift_tokens(dst, src, done):
                    nc.scalar.copy(dst[0:DH, :], src[0:DH])
                    nc.scalar.copy(dst[DH:P, 1:SEQ], src[DH:P, 0:SEQ - 1]).then_inc(done, 1)
                shift_tokens(xs, xT[:, b, :], S["xs_ready"])

                def project(t):
                    for side in range(2):
                        filled(act, it, "qk"[side] + str(t))
                        act.wait_ge(S["sumsq"], it * TPB + t)
                        nc.scalar.activation(sq[:, side].rearrange("p h d -> p (h d)"),
                                             slot("qk"[side] + str(t))[:, :, :].rearrange("p a n -> p (a n)"),
                                             ACT.Square).then_inc(S["squares"], 1)
                    filled(act, it, f"v{t}")
                    nc.scalar.copy(va[:, t, :, 0:DH], slot(f"v{t}")[:, :, :].rearrange("p a n -> p (a n)").rearrange(
                        "p (h d) -> p h d", d=DH)).then_inc(S["act_read"], 1)

                def move(what, dst):
                    filled(act, it, what)
                    nc.scalar.copy(dst, slot(what)[:, :, :].rearrange("p a n -> p (a n)").rearrange(
                        "p (c n) -> p c n", n=P)).then_inc(S["act_read"], 1)

                def feed_forward():
                    was_read(act, it, "wo")
                    shift_tokens(xs2, x1, S["xs2_ready"])
                    was_read(act, it, "mean")
                    nc.scalar.activation(sqc[:, :], xc[:, :], ACT.Square).then_inc(S["centered_sq"], 1)
                    filled(act, it, "var")
                    nc.scalar.activation(sqc[:, :], slot("var")[:, 0, :], ACT.Sqrt, bias=epsc[:, 0:1]).then_inc(S["act_read"], 1)
                    for j in range(NJ):
                        filled(act, it, f"f{j}")
                        if j:
                            was_read(act, it, f"f{j - 1}")
                        nc.scalar.activation(gate[:, :], slot(f"f{j}")[0:JW, 1, :], ACT.Gelu,
                                             bias=b_1[:, 1, j:j + 1]).then_inc(S["gates"], 1)

                for stage in ORDER:
                    t = int(stage[1:] or 0)
                    if stage[0] == "P":
                        project(t)
                    elif stage[0] == "T":
                        move(f"qT{t}", qT[:, :, t * P:(t + 1) * P])
                        move(f"kT{t}", kT[:, :, WIN + t * P:WIN + (t + 1) * P])
                    elif stage[0] == "S":
                        was_read(act, it, f"s{t}")
                        nc.scalar.activation(prob[:, :, :], prob[:, :, :], ACT.Exp).then_inc(S["probs"], 1)
                    elif stage[0] == "R":
                        move(f"r{t}", probT[:, :, :])
                    elif stage[0] == "O":
                        move(f"o{t}", oT[:, :, t * P:(t + 1) * P])
                    elif stage[0] == "C":
                        feed_forward()
            units(act, layer_start, body)

        @block.tensor
        def _(pe):
            pe.wait_ge(S["const_ready"], 9)

            def layer_start(l):
                pe.wait_ge(S["weights"], 16 * NW * (l + 1))
                passed(pe)

            def body(it, l, b):
                def free(what):
                    before = FILL[what] - SLOTS_PS
                    if before >= 0:
                        was_read(pe, it, BY_FILL[before])

                def project(t):
                    for side, name in enumerate(("q", "k", "v")):
                        free(name + str(t))
                        for i in range(2):
                            last = nc.tensor.matmul(slot(name + str(t))[:, i, :], xs[:, t * P:(t + 1) * P],
                                                    w_qkv[:, side, i * SEQ:(i + 1) * SEQ], start=True, stop=True)
                        last.then_inc(S["filled"], 1)

                def transposes(what, src):
                    free(what)
                    dst = slot(what)[:, :, :].rearrange("p a n -> p (a n)")
                    for c in range(8):
                        last = nc.tensor.transpose(dst[:, c * P:(c + 1) * P], src[:, c * P:(c + 1) * P], ident[:, :])
                    last.then_inc(S["filled"], 1)

                def scores(t):
                    free(f"s{t}")
                    was_read(pe, it, f"kT{t}")
                    ps = slot(f"s{t}")
                    for half in range(2):
                        nc.tensor.matmul(ps[:, half, :], ident16[:, :], mask[:, 0 if t == 0 else 1, :],
                                         start=True, stop=False, skip_group_check=True)
                        for hg in (2 * half, 2 * half + 1):
                            for n, w in enumerate((4 * t + 1, 4 * t + 3, 4 * t, 4 * t + 2)):
                                for g in range(4):
                                    h = 4 * hg + g
                                    r = DH * (h % 2)
                                    col = (hg % 2) * 4 * DH + n * DH
                                    last = nc.tensor.matmul(
                                        ps[32 * g:32 * g + 32, half, col:col + DH],
                                        qT[r:r + DH, h // 2, WIN * w:WIN * w + WIN],
                                        kT[r:r + DH, h // 2, WIN * w:WIN * w + 2 * WIN],
                                        start=False, stop=True, skip_group_check=True)
                    last.then_inc(S["filled"], 1)

                def products(t):
                    was_read(pe, it, f"r{t}")
                    pe.wait_ge(vb_ready[t], (16 if t == 0 else 32) * (it + 1))
                    for k, name in enumerate((f"va{t}", f"vb{t}")):
                        free(name)
                        passed(pe)
                        for a in range(2):
                            hg = 2 * k + a
                            for g in range(4):
                                h = 4 * hg + g
                                for n, (w, src, half) in enumerate(((1, va, 0), (3, va, 1), (0, vb, 0), (2, vb, 1))):
                                    r = DH * half
                                    last = nc.tensor.matmul(
                                        slot(name)[32 * w:32 * w + 32, a, g * VA:(g + 1) * VA],
                                        probT[r:r + DH, 2 * hg + n // 2, 32 * g:32 * g + 32],
                                        src[r:r + DH, t, h, :], start=True, stop=True, skip_group_check=True)
                        last.then_inc(S["filled"], 1)

                def feed_forward():
                    free("wo")
                    was_read(pe, it, f"o{TPB - 1}")
                    for c in range(QCH):
                        last = nc.tensor.matmul(slot("wo")[:, 0, :], w_o[:, c, :], oT[:, c, :], start=c == 0, stop=c == QCH - 1)
                    last.then_inc(S["filled"], 1)
                    free("mean")
                    pe.wait_ge(S["xs2_ready"], it + 1)
                    nc.tensor.matmul(slot("mean")[:, 0, :], ones[:, :], xs2[:, :], start=True, stop=True).then_inc(S["filled"], 1)
                    free("var")
                    pe.wait_ge(S["centered_sq"], it + 1)
                    nc.tensor.matmul(slot("var")[:, 0, :], ones[:, :], sqc[:, :], start=True, stop=True).then_inc(S["filled"], 1)
                    pe.wait_ge(S["link"], (it + 1) * (TPB * 18 + 3))
                    for j in range(NJ):
                        free(f"f{j}")
                        for a in (1, 0):
                            last = nc.tensor.matmul(slot(f"f{j}")[0:JW, a, :], w_1[:, a, j, :], z[:, :], start=True, stop=True)
                        last.then_inc(S["filled"], 1)
                    free("y")
                    for j in range(NJ):
                        was_read(pe, it, f"f{j}")
                        last = nc.tensor.matmul(slot("y")[:, 0, :], w_2[:, j, :], hid[:, j, :], start=j == 0, stop=j == NJ - 1)
                    last.then_inc(S["filled"], 1)
                    was_read(pe, it, "y")

                pe.wait_ge(S["xs_ready"], it + 1)
                for stage in ORDER:
                    t = int(stage[1:] or 0)
                    if stage[0] == "P":
                        project(t)
                    elif stage[0] == "T":
                        for side, name in enumerate((f"qT{t}", f"kT{t}")):
                            pe.wait_ge(S["normed"], it * 8 + 2 * t + side + 1)
                            transposes(name, qk[:, side].rearrange("p h d -> p (h d)"))
                    elif stage[0] == "S":
                        scores(t)
                    elif stage[0] == "R":
                        pe.wait_ge(S["probs"], it * TPB + t + 1)
                        transposes(f"r{t}", prob[:, :, :].rearrange("p h d -> p (h d)"))
                    elif stage[0] == "V":
                        products(t)
                    elif stage[0] == "O":
                        was_read(pe, it, f"vb{t}")
                        transposes(f"o{t}", o[:, :, :].rearrange("p h d -> p (h d)"))
                    elif stage[0] == "C":
                        feed_forward()
            units(pe, layer_start, body)


def add_up(nc, io, xT, ident):
    with ExitStack() as ctx:
        res = ctx.enter_context(nc.sbuf_tensor("fin_res", [P, TILES, D], F32))
        fetched = ctx.enter_context(nc.semaphore("fin_fetched"))
        sem = lambda n: ctx.enter_context(nc.semaphore(n))
        ps = [ctx.enter_context(nc.psum_tensor(f"fin_ps{i}", [P, 4 * P], F32)) for i in range(2)]
        turned, summed, stored = sem("fin_turned"), sem("fin_summed"), sem("fin_stored")
        block = ctx.enter_context(nc.Block())

        @block.tensor
        def _(pe):
            for b in range(BATCH):
                if b >= 2:
                    pe.wait_ge(summed, b - 1)
                for t in range(TPB):
                    last = nc.tensor.transpose(ps[b % 2][:, t * P:(t + 1) * P], xT[:, b, t * P:(t + 1) * P], ident[:, :])
                last.then_inc(turned, 1)

        @block.vector
        def _(dve):
            dve.wait_ge(fetched, 16)
            for b in range(BATCH):
                dve.wait_ge(turned, b + 1)
                r = res[:, TPB * b:TPB * (b + 1), :]
                nc.vector.tensor_tensor(r, r, ps[b % 2][:, :].rearrange("p (t d) -> p t d", d=D), ALU.add).then_inc(summed, 1)

        @block.sync
        def _(sp):
            sp.dma_start(res[:, :, :], io["kept"].rearrange("(n p) d -> p n d", p=P)).then_inc(fetched, 16)
            out = io["out"].rearrange("(n p) d -> p n d", p=P)
            for b in range(BATCH):
                sp.wait_ge(summed, b + 1)
                sp.dma_start(out[:, TPB * b:TPB * (b + 1), :], res[:, TPB * b:TPB * (b + 1), :]).then_inc(stored, 16)
            sp.wait_ge(stored, 16 * BATCH)


def build(nc, io):
    with nc.sbuf_tensor("xT", [P, BATCH, SEQ], F32) as xT, nc.sbuf_tensor("ident", [P, P], F32) as ident:
        with nc.sbuf_tensor("res", [P, TILES, D], F32) as res:
            layer_norm_and_transpose(nc, io, res, xT, ident)
            global_attention(nc, io, res, xT, ident)
        windowed_stack(nc, io, xT, ident)
        add_up(nc, io, xT, ident)


def rotation_tables():
    half = np.arange(0, DH, 2, dtype=np.float64)
    t = np.arange(SEQ, dtype=np.float64)
    freqs = t[:, None] * (1.0 / 10000.0 ** (half / DH))[None, :]
    scale = ((half + 0.4 * DH) / (1.4 * DH))[None, :] ** ((t - SEQ // 2) / (WIN // 2))[:, None]
    sign = np.concatenate([-np.ones(DH // 2), np.ones(DH // 2)])
    two = lambda a: np.concatenate([a, a], -1)
    cos, sin, scale = two(np.cos(freqs)), two(np.sin(freqs)) * sign, two(scale)
    kinds = np.stack([8.0 * cos * scale, 8.0 * sin * scale, cos / scale, sin / scale], 1)
    return np.ascontiguousarray(kinds.reshape(TPB, P, 4, DH).transpose(1, 0, 2, 3).astype(np.float32))


def window_masks():
    i = np.arange(P)[:, None] % WIN
    j = np.arange(2 * WIN)[None, :]
    block = np.where((j >= i) & (j <= i + WIN), 0.0, MASKED)
    first = np.where((j >= WIN) & (j <= i + WIN), 0.0, MASKED)
    rows = lambda w0: np.tile(np.concatenate([block, block, w0, block], 1), (1, 2))
    return np.ascontiguousarray(np.stack([rows(first), rows(block)], 1).astype(np.float32))


def kernel(**inputs):
    import concourse.bacc as bacc
    from concourse.bass_utils import run_bass_kernel_spmd

    f = {k[3:]: np.asarray(v) for k, v in inputs.items()}
    w = f["attn_Wqkv"].reshape(CH, 3, HD, D).transpose(3, 1, 0, 2).reshape(D, 3 * D)
    bq = f["attn_bqkv"].reshape(CH, 3, HD).transpose(1, 0, 2).reshape(1, 3 * D)
    w1 = np.zeros((DEPTH, D, 2, NJ * JW), np.float32)
    w1[:, :, :, :DIN] = f["ffn_W1"].reshape(DEPTH, D, 2, DIN)
    b1 = np.zeros((DEPTH, 2, NJ * JW), np.float32)
    b1[:, :, :DIN] = f["ffn_b1"].reshape(DEPTH, 2, DIN)
    w2 = np.zeros((DEPTH, NJ * JW, D), np.float32)
    w2[:, :DIN] = f["ffn_W2"]
    scales = np.concatenate([f["ffn_q_scale"], f["ffn_k_scale"]], 1)[:, None, :]
    arrays = {
        "x": f["attn_x"].reshape(TOKENS, D),
        "ident": np.eye(P, dtype=np.float32),
        "bo_rows": np.broadcast_to(f["attn_bo"], (P, D)),
        "at_wqkvT": w,
        "at_woT": f["attn_Wo"].T,
        "at_bias": np.broadcast_to(bq, (P, 3 * D)),
        "rot": rotation_tables(),
        "mask": window_masks(),
        "w_qkv": f["ffn_Wqkv"],
        "qk_scale": np.broadcast_to(scales, (DEPTH, P, 2 * DH)),
        "w_o": f["ffn_Wo"],
        "w_1": w1.reshape(DEPTH, D, 2 * NJ * JW),
        "w_2": w2,
        "b_1": b1.reshape(DEPTH, 2, NJ, JW).transpose(0, 3, 1, 2).reshape(DEPTH, JW, 2 * NJ),
        "vec": np.stack([f["ffn_ln_g"], f["ffn_ln_b"], f["ffn_b2"]], 2),
    }
    arrays = {f"in_{k}": np.ascontiguousarray(v) for k, v in arrays.items()}
    nc = bacc.Bacc("TRN2", target_bir_lowering=False, num_devices=1)
    io = {k[3:]: nc.dram_tensor(k, v.shape, F32, kind="ExternalInput").ap() for k, v in arrays.items()}
    io["out"] = nc.dram_tensor("out_0", (TOKENS, D), F32, kind="ExternalOutput").ap()
    io["kept"] = nc.dram_tensor("kept", (TOKENS, D), F32, kind="Internal").ap()
    build(nc, io)
    r = run_bass_kernel_spmd(nc, [arrays], core_ids=[0])
    return r.results[0]["out_0"].reshape(BATCH, SEQ, D)
```

```python
import numpy as np
import concourse.bass as bass
from concourse import mybir
from contextlib import ExitStack

F32 = mybir.dt.float32
BF16 = mybir.dt.bfloat16
I32 = mybir.dt.int32
ALU = mybir.AluOpType
ACT = mybir.ActivationFunctionType
AX = mybir.AxisListType

P = 128
D = 128
BATCH, SEQ = 8, 512
TOKENS = BATCH * SEQ
TILES = TOKENS // P
HEADS = 16

HD = D // HEADS
CH = SEQ // 32
HPT = P // 32
SLOTS = 64
SHIFT_ROW = 6 * HD

DEPTH, DH, WIN = 6, 64, 32
INNER = HEADS * DH
QCH = INNER // P
DIN = int(D * 4 * 2 / 3)
NJ = 3
JW = (DIN + NJ - 1) // NJ
TPB = SEQ // P
EPS = 1e-5
MASKED = -1.0e30
VA = DH + 1


def layer_norm_and_transpose(nc, io, res, xT, ident):
    with ExitStack() as ctx:
        sb = lambda n, s, d=F32: ctx.enter_context(nc.sbuf_tensor(n, s, d))
        sem = lambda n: ctx.enter_context(nc.semaphore(n))
        xn = sb("ln_xn", [P, TILES, D])
        stats = sb("ln_stats", [P, TILES, 6])
        agg = sb("ln_agg", [P, TILES, 2])
        std = sb("ln_std", [P, TILES])
        rstd = sb("ln_rstd", [P, TILES])
        bo = sb("ln_bo", [P, D])
        ps = [ctx.enter_context(nc.psum_tensor(f"ln_ps{i}", [P, 4 * P], F32)) for i in range(2)]
        loaded, stats_done, agg_done, std_done, rstd_done, xn_done, moved, transposed = map(
            sem, ("ln_loaded", "ln_stats_done", "ln_agg_done", "ln_std_done", "ln_rstd_done", "ln_xn_done",
                  "ln_moved", "ln_transposed"))
        block = ctx.enter_context(nc.Block())

        @block.sync
        def _(sp):
            sp.dma_start(res[:, :, :], io["x"].rearrange("(n p) d -> p n d", p=P)).then_inc(loaded, 16)
            sp.dma_start(ident[:, :], io["ident"]).then_inc(loaded, 16)
            sp.dma_start(bo[:, :], io["bo_rows"]).then_inc(loaded, 16)

        @block.vector
        def _(dve):
            dve.wait_ge(loaded, 48)
            for i in range(TILES):
                nc.vector.bn_stats(stats[:, i, :], res[:, i, :]).then_inc(stats_done, 1)
            for i in range(TILES):
                dve.wait_ge(stats_done, i + 1)
                nc.vector.bn_aggr(agg[:, i, :], stats[:, i, :]).then_inc(agg_done, 1)
            dve.wait_ge(agg_done, TILES)
            nc.vector.tensor_scalar(std[:, :], agg[:, :, 1], EPS, None, ALU.add).then_inc(agg_done, 1)
            dve.wait_ge(std_done, 1)
            nc.vector.reciprocal(rstd[:, :], std[:, :]).then_inc(rstd_done, 1)
            dve.wait_ge(rstd_done, 1)
            for i in range(TILES):
                nc.vector.tensor_scalar(xn[:, i, :], res[:, i, :], agg[:, i, 0:1], rstd[:, i:i + 1],
                                        ALU.subtract, ALU.mult).then_inc(xn_done, 1)
            dve.wait_ge(xn_done, TILES)
            nc.vector.tensor_tensor(res[:, :, :], res[:, :, :],
                                    bo[:, None, :].broadcast_to([P, TILES, D]), ALU.add).then_inc(xn_done, 1)

        @block.scalar
        def _(act):
            act.wait_ge(agg_done, TILES + 1)
            nc.scalar.activation(std[:, :], std[:, :], ACT.Sqrt).then_inc(std_done, 1)
            for b in range(BATCH):
                act.wait_ge(transposed, b + 1)
                nc.scalar.copy(xT[:, b, :], ps[b % 2][:, :]).then_inc(moved, 1)

        @block.tensor
        def _(pe):
            for b in range(BATCH):
                pe.wait_ge(xn_done, TPB * (b + 1))
                if b >= 2:
                    pe.wait_ge(moved, b - 1)
                for t in range(TPB):
                    last = nc.tensor.transpose(ps[b % 2][:, t * P:(t + 1) * P], xn[:, TPB * b + t, :], ident[:, :])
                last.then_inc(transposed, 1)


def global_attention(nc, io, res, xT, ident):
    with ExitStack() as ctx:
        sb = lambda n, s, d=F32: ctx.enter_context(nc.sbuf_tensor(n, s, d))
        sem = lambda n: ctx.enter_context(nc.semaphore(n))
        w_qkv = sb("at_wqkv", [P, 3 * P])
        w_o = sb("at_wo", [P, P])
        bias = sb("at_bias", [P, 3 * P])
        ident16 = sb("at_ident16", [P, P], BF16)
        xg = sb("at_xg", [P, P])
        qkv = sb("at_qkv", [P, 3, CH, HD])
        part = sb("at_part", [P, 3, 2, CH, HD], BF16)
        rest = sb("at_rest", [P, 2, CH, HD])
        stack = sb("at_stack", [P, 2, CH, SLOTS], BF16)
        qs = [sb(f"at_qs{i}", [P, HPT, CH, 32], BF16) for i in range(2)]
        ks = [sb(f"at_ks{i}", [P, HPT, CH, 32], BF16) for i in range(2)]
        vs = [sb(f"at_vs{i}", [P, HPT, 4, 32]) for i in range(2)]
        rowmax = sb("at_rowmax", [P, HPT * 4])
        mrest = sb("at_mrest", [P, HPT * 4])
        mpart = sb("at_mpart", [P, 3, HPT * 4], BF16)
        mT = sb("at_mT", [3 * HPT * 4, P], BF16)
        probs = [sb(f"at_probs{i}", [P, 2, SEQ]) for i in range(2)]
        oT = sb("at_oT", [P, CH, 32])
        rden = sb("at_rden", [P, CH])
        vals = sb("at_vals", [P, CH, HD])
        valsT = sb("at_valsT", [P, P])
        ps_exp = [ctx.enter_context(nc.psum_tensor(f"at_pe{i}", [P, 2, SEQ], F32)) for i in range(2)]
        ps_max = [ctx.enter_context(nc.psum_tensor(f"at_pm{i}", [P, SEQ], F32)) for i in range(2)]
        ps_o = ctx.enter_context(nc.psum_tensor("at_po", [P, SEQ], F32))
        ps_x = ctx.enter_context(nc.psum_tensor("at_px", [P, SEQ], F32))
        names = ("loaded", "cleared", "ident_done", "x_taken", "projected", "biased", "parted", "v_placed", "stacked",
                 "stack_transposed", "stack_moved", "scored_max", "max_done", "mpart_done", "m_transposed", "m_moved",
                 "shift_rows", "scored_exp", "exp_done", "pv_done", "o_taken", "rden_done", "vals_done", "vals_transposed",
                 "vals_moved", "y_done", "res_done", "link", "passed", "kept")
        S = {n: sem("at_" + n) for n in names}
        block = ctx.enter_context(nc.Block())
        SCALE = 1.0 / float(np.sqrt(HD))

        def passed(eng):
            eng.sem_inc(S["passed"], 1)

        def groups(eng, front, back):
            front(0, 0, None, None)
            with eng.Fori(0, TILES // 2 - 1) as i:
                front(2 * i + 1, 1, 2 * i, 0)
                front(2 * i + 2, 0, 2 * i + 1, 1)
            front(TILES - 1, 1, TILES - 2, 0)
            back(TILES - 1, 1)

        @block.sync
        def _(sp):
            sp.dma_start(w_qkv[:, :], io["at_wqkvT"]).then_inc(S["loaded"], 16)
            sp.dma_start(w_o[:, :], io["at_woT"]).then_inc(S["loaded"], 16)
            sp.dma_start(bias[:, :], io["at_bias"]).then_inc(S["loaded"], 16)

            def shift(g, par):
                sp.wait_ge(S["m_moved"], g + 1)
                sp.dma_start(qs[par][SHIFT_ROW:SHIFT_ROW + 3, :, :, :].rearrange("p h c t -> p (h c t)")
                             .rearrange("p (r q) -> p r q", q=P),
                             mT[:, :]).then_inc(S["shift_rows"], 16)
                sp.wait_ge(S["shift_rows"], 16 * g + 16)
                passed(sp)
            with sp.Fori(0, TILES // 2) as i:
                shift(2 * i, 0)
                shift(2 * i + 1, 1)
            sp.wait_ge(S["res_done"], TILES)
            sp.dma_start(io["kept"].rearrange("(n p) d -> p n d", p=P), res[:, :, :]).then_inc(S["kept"], 16)
            sp.wait_ge(S["kept"], 16)

        @block.gpsimd
        def _(pool):
            pool.memset(stack[:, :, :, :], 0.0).then_inc(S["cleared"], 1)
            pool.wait_ge(S["cleared"], 1)
            pool.memset(stack[:, 1, :, SHIFT_ROW:SHIFT_ROW + 3], 1.0).then_inc(S["cleared"], 1)
            pool.memset(ks[0][:, :, :, :], 0.0).then_inc(S["cleared"], 1)
            pool.memset(ks[1][:, :, :, :], 0.0).then_inc(S["cleared"], 1)
            pool.memset(qs[0][:, :, :, :], 0.0).then_inc(S["cleared"], 1)
            pool.memset(qs[1][:, :, :, :], 0.0).then_inc(S["cleared"], 1)
            for v in vs:
                pool.memset(v[:, :, :, :], 0.0).then_inc(S["cleared"], 1)
            pool.wait_ge(S["cleared"], 8)
            for v in vs:
                pool.memset(v[:, :, :, HD:HD + 1], 1.0).then_inc(S["cleared"], 1)
            pool.wait_ge(S["cleared"], 10)

            def place(g, *_):
                pool.wait_ge(S["parted"], g + 1)
                pool.wait_ge(S["stack_transposed"], 4 * g)
                passed(pool)
                for side, slot, p in ((0, 0, 0), (0, 1, 0), (0, 2, 1), (0, 3, 0), (0, 4, 1), (0, 5, 2),
                                      (1, 0, 0), (1, 1, 1), (1, 2, 0), (1, 3, 2), (1, 4, 1), (1, 5, 0)):
                    last = nc.gpsimd.tensor_scalar(stack[:, side, :, slot * HD:(slot + 1) * HD],
                                                   part[:, p, side, :, :], 1.0, 0.0, ALU.mult, ALU.add)
                last.then_inc(S["stacked"], 1)
            with pool.Fori(0, TILES) as g:
                place(g)

        @block.vector
        def _(dve):
            dve.wait_ge(S["loaded"], 48)
            nc.vector.tensor_copy(ident16[:, :], ident[:, :]).then_inc(S["ident_done"], 1)
            dve.wait_ge(S["cleared"], 10)
            LINKS = 9

            def front(g, par, gb, parb):
                links = [0]

                def link(ins):
                    links[0] += 1
                    ins.then_inc(S["link"], 1)
                    dve.wait_ge(S["link"], g * LINKS + links[0])
                dve.wait_ge(S["projected"], g + 1)
                nc.vector.tensor_tensor(qkv[:, :, :, :].rearrange("p a c d -> p (a c d)"), ps_x[:, 0:3 * P],
                                        bias[:, :], ALU.add).then_inc(S["biased"], 1)
                dve.wait_ge(S["biased"], g + 1)
                dve.wait_ge(S["stacked"], g)
                link(nc.vector.tensor_copy(part[:, 0], qkv[:, 0:2]))
                link(nc.vector.tensor_tensor(rest[:, :], qkv[:, 0:2], part[:, 0], ALU.subtract))
                link(nc.vector.tensor_copy(part[:, 1], rest[:, :]))
                nc.vector.tensor_tensor(part[:, 2], rest[:, :], part[:, 1], ALU.subtract).then_inc(S["parted"], 1)
                if gb is not None:
                    dve.wait_ge(S["pv_done"], 4 * gb)
                for h in range(HPT):
                    for c4 in range(4):
                        last = nc.vector.tensor_copy(
                            vs[par][32 * c4:32 * c4 + 32, h, :, 0:HD],
                            qkv[32 * h:32 * h + 32, 2, :, :].rearrange("p (b c) d -> p b c d", c=4)[:, :, c4, :])
                last.then_inc(S["v_placed"], 1)
                for h in range(HPT):
                    for qc in range(4):
                        k = 4 * h + qc
                        dve.wait_ge(S["scored_max"], 16 * g + k + 1)
                        nc.vector.reduce_max(rowmax[:, k:k + 1], ps_max[k % 2][:, :], AX.X).then_inc(S["max_done"], 1)
                dve.wait_ge(S["max_done"], 16 * g + 16)
                dve.wait_ge(S["m_transposed"], g)
                link(nc.vector.tensor_scalar(mrest[:, :], rowmax[:, :], -1.0, None, ALU.mult))
                link(nc.vector.tensor_copy(mpart[:, 0, :], mrest[:, :]))
                link(nc.vector.tensor_tensor(mrest[:, :], mrest[:, :], mpart[:, 0, :], ALU.subtract))
                link(nc.vector.tensor_copy(mpart[:, 1, :], mrest[:, :]))
                link(nc.vector.tensor_tensor(mrest[:, :], mrest[:, :], mpart[:, 1, :], ALU.subtract))
                link(nc.vector.tensor_copy(mpart[:, 2, :], mrest[:, :]))
                assert links[0] == LINKS, links
                if gb is not None:
                    back(gb, parb)

            def back(g, par):
                dve.wait_ge(S["pv_done"], 4 * g + 4)
                nc.vector.transpose(oT[:, :, :].rearrange("p c d -> p (c d)"), ps_o[:, :]).then_inc(S["o_taken"], 1)
                dve.wait_ge(S["o_taken"], g + 1)
                nc.vector.reciprocal(rden[:, :], oT[:, :, HD]).then_inc(S["rden_done"], 1)
                dve.wait_ge(S["rden_done"], g + 1)
                nc.vector.tensor_tensor(vals[:, :, :], oT[:, :, 0:HD], rden[:, :, None].broadcast_to([P, CH, HD]),
                                        ALU.mult).then_inc(S["vals_done"], 1)
                dve.wait_ge(S["y_done"], g + 1)
                nc.vector.tensor_tensor(res[:, g, :], res[:, g, :], ps_x[:, 0:P], ALU.add).then_inc(S["res_done"], 1)
            groups(dve, front, back)

        @block.scalar
        def _(act):
            act.wait_ge(S["cleared"], 10)

            def exps(g, h, par):
                for pair in range(2):
                    k = 2 * h + pair
                    act.wait_ge(S["scored_exp"], 8 * g + k + 1)
                    act.wait_ge(S["pv_done"], 4 * g + h)
                    nc.scalar.activation(probs[pair][:, :, :], ps_exp[pair][:, :, :], ACT.Exp,
                                         scale=SCALE).then_inc(S["exp_done"], 1)

            def finish(g):
                act.wait_ge(S["vals_transposed"], g + 1)
                nc.scalar.copy(valsT[:, :], ps_x[:, 0:P]).then_inc(S["vals_moved"], 1)

            def front(g, par, gb, parb):
                act.wait_ge(S["projected"], g)
                nc.scalar.copy(xg[:, :], xT[:, :, :].rearrange("p b s -> p (b s)")[:, bass.ts(g, P)]).then_inc(S["x_taken"], 1)
                for j in range(4):
                    side, half = j // 2, j % 2
                    act.wait_ge(S["stack_transposed"], 4 * g + j + 1)
                    dst = (qs, ks)[side][par][0:SLOTS, :, half * 8:half * 8 + 8, :].rearrange("p h c t -> p c h t")
                    src = ps_max[j % 2][:, :].bitcast(BF16)[0:SLOTS, :].rearrange("p (c h t) -> p c h t", h=HPT, t=32)
                    nc.scalar.copy(dst, src).then_inc(S["stack_moved"], 1)
                if gb is not None:
                    for h in range(HPT):
                        exps(gb, h, parb)
                act.wait_ge(S["shift_rows"], 16 * g)
                act.wait_ge(S["m_transposed"], g + 1)
                nc.scalar.copy(mT[:, :], ps_x[:, 0:P // 2].bitcast(BF16)[0:3 * HPT * 4, :]).then_inc(S["m_moved"], 1)
                if gb is not None:
                    finish(gb)

            def back(g, par):
                for h in range(HPT):
                    exps(g, h, par)
                finish(g)
            groups(act, front, back)

        @block.tensor
        def _(pe):
            pe.wait_ge(S["ident_done"], 1)
            pe.wait_ge(S["cleared"], 10)

            def exp_head(g, h, par):
                for pair in range(2):
                    k = 2 * h + pair
                    pe.wait_ge(S["exp_done"], 8 * g + k - 1 if h else 8 * g)
                    for i in range(2):
                        kc = 2 * pair + i
                        last = nc.tensor.matmul(
                            ps_exp[pair][:, i, :],
                            ks[par][:, h, :, :].rearrange("p c t -> p (c t)")[:, kc * P:(kc + 1) * P],
                            qs[par][:, h, :, :].rearrange("p c t -> p (c t)"), start=True, stop=True)
                    last.then_inc(S["scored_exp"], 1)
                if h == 0:
                    pe.wait_ge(S["v_placed"], g + 1)
                    pe.wait_ge(S["o_taken"], g)
                for pair in range(2):
                    pe.wait_ge(S["exp_done"], 8 * g + 2 * h + pair + 1)
                    for i in range(2):
                        kc = 2 * pair + i
                        last = nc.tensor.matmul(ps_o[32 * h:32 * h + 32, :], vs[par][:, h, kc, :], probs[pair][:, i, :],
                                                start=kc == 0, stop=kc == 3)
                last.then_inc(S["pv_done"], 1)

            def max_head(g, h, par):
                for qc in range(4):
                    k = 4 * h + qc
                    if k < 2:
                        pe.wait_ge(S["stack_moved"], 4 * g + 4)
                    else:
                        pe.wait_ge(S["max_done"], 16 * g + k - 1)
                    nc.tensor.matmul(ps_max[k % 2][:, :],
                                     qs[par][:, h, :, :].rearrange("p c t -> p (c t)")[:, qc * P:(qc + 1) * P],
                                     ks[par][:, h, :, :].rearrange("p c t -> p (c t)"),
                                     start=True, stop=True).then_inc(S["scored_max"], 1)

            def finish(g):
                pe.wait_ge(S["vals_done"], g + 1)
                nc.tensor.transpose(ps_x[:, 0:P], vals[:, :, :].rearrange("p c d -> p (c d)"), ident[:, :]).then_inc(S["vals_transposed"], 1)
                pe.wait_ge(S["vals_moved"], g + 1)
                nc.tensor.matmul(ps_x[:, 0:P], valsT[:, :], w_o[:, :], start=True, stop=True).then_inc(S["y_done"], 1)

            def front(g, par, gb, parb):
                pe.wait_ge(S["x_taken"], g + 1)
                if gb is not None:
                    pe.wait_ge(S["res_done"], gb)
                    pe.wait_ge(S["m_moved"], g)
                nc.tensor.matmul(ps_x[:, 0:3 * P], xg[:, :], w_qkv[:, :], start=True, stop=True).then_inc(S["projected"], 1)
                pe.wait_ge(S["stacked"], g + 1)
                for j in range(4):
                    side, half = j // 2, j % 2
                    if j < 2:
                        pe.wait_ge(S["max_done"], 16 * g)
                    else:
                        pe.wait_ge(S["stack_moved"], 4 * g + j - 1)
                    passed(pe)
                    for c in range(8):
                        last = nc.tensor.transpose(ps_max[j % 2][:, :].bitcast(BF16)[0:SLOTS, c * P:(c + 1) * P],
                                                   stack[:, side, 8 * half + c, :], ident16[:, :])
                    last.then_inc(S["stack_transposed"], 1)
                if gb is not None:
                    pe.wait_ge(S["shift_rows"], 16 * gb + 16)
                for h in range(HPT):
                    max_head(g, h, par)
                    if gb is not None:
                        exp_head(gb, h, parb)
                pe.wait_ge(S["biased"], g + 1)
                pe.wait_ge(S["link"], g * 9 + 9)
                passed(pe)
                nc.tensor.transpose(ps_x[:, 0:P // 2].bitcast(BF16)[0:3 * HPT * 4, :],
                                    mpart[:, :, :].rearrange("p a b -> p (a b)"), ident16[:, :]).then_inc(S["m_transposed"], 1)
                if gb is not None:
                    pe.wait_ge(S["m_moved"], g + 1)
                    finish(gb)

            def back(g, par):
                pe.wait_ge(S["shift_rows"], 16 * g + 16)
                for h in range(HPT):
                    exp_head(g, h, par)
                pe.wait_ge(S["res_done"], g)
                finish(g)
            groups(pe, front, back)


def stages(text):
    out = []
    for word in text.split():
        name = word.rstrip("-")
        kind = name.rstrip("0123456789")
        out.append((kind, int(name[len(kind):] or 0), len(word) - len(name)))
    return out


PE_ORDER = stages(
    "s2- r1- kT3- k0 qT3- va1- q0 o0- vb1- r2- s3- o1- va2- vb2- q1 o2- r3- k1 qT0 va3- kT0 vb3- v0 o3- s0 wo- k2 "
    "r0 q2 va0 kT1 mean- v1 v2 var- vb0 v3 k3 qT1 h0- q3 h1- s1 h2- qT2 kT2 y- ")
DVE_ORDER = stages(
    "scale_q3- s2- rotate_k0 va1- norms0 vb1- rotate_q0 s3- vb2- va2- scale_k0 scale_q0 rotate_q1 rotate_k1 va3- "
    "vb3- norms1 s0 scale_k1 scale_q1 residual- rotate_k2 va0 center- rotate_q2 norms2 z- vb0 scale_k2 rotate_k3 hid0- "
    "scale_q2 hid1- rotate_q3 norms3 hid2- s1 y- scale_k3 ")
ACT_ORDER = stages(
    "r1- kT3- square_k0 qT3- exp2- square_q0 o0- r2- o1- exp3- square_q1 o2- r3- square_k1 qT0 kT0 v0 o3- exp0 "
    "square_k2 r0 shift- square_q2 kT1 square- v1 root- v2 square_k3 qT1 gate0- square_q3 gate1- v3 gate2- qT2 kT2 "
    "exp1 next ")
POOL_ORDER = stages(
    "add_q3- add_k0 root0 add_q0 add_q1 root1 add_k1 add_k2 root2 add_q2 add_k3 root3 ")
SP_ORDER = stages(
    "vb2- vb3- vb0 vb1 ")
SLOTS_OF = (
    "kT0 r0 va0 q1 v1 va1 s2 v3 s3 o3 wo h2",
    "q0 s0 vb0 k1 s1 q2 vb2 kT3 h0",
    "k0 v0 qT1 vb1 o1 k2 v2 kT2 q3 r3 va3 mean",
    "qT0 o0 kT1 r1 qT2 r2 va2 o2 k3 qT3 vb3 var h1 y",)

FILLS = {"q": (TPB, "dve"), "k": (TPB, "dve"), "v": (TPB, "act"), "qT": (TPB, "act"), "kT": (TPB, "act"),
         "s": (TPB, "dve"), "r": (TPB, "act"), "va": (TPB, "dve"), "vb": (TPB, "dve"), "o": (TPB, "act"),
         "wo": (1, "dve"), "mean": (1, "dve"), "var": (1, "act"), "h": (NJ, "dve"), "y": (1, "dve")}
EVENTS = {"q_squared": ("act", TPB), "k_squared": ("act", TPB), "sumsq": ("dve", TPB), "seeded": ("dve", TPB),
          "q_added": ("pool", TPB), "k_added": ("pool", TPB), "rooted": ("pool", TPB),
          "q_scaled": ("dve", TPB), "k_scaled": ("dve", TPB), "probs": ("act", TPB),
          "xs2_ready": ("act", 1), "centered_sq": ("act", 1), "z_ready": ("dve", 1), "gates": ("act", NJ)}
EVENTS.update({kind + "_filled": ("pe", n) for kind, (n, _) in FILLS.items()})
EVENTS.update({kind + "_read": (engine, n) for kind, (n, engine) in FILLS.items()})
SLOT = {(kind, n): k for k, names in enumerate(SLOTS_OF) for kind, n, _ in stages(names)}
PROJECTIONS = [(kind, n) for kind, n, _ in PE_ORDER if kind in ("q", "k", "v")]
ROTATIONS = [(kind, n) for kind, n, _ in DVE_ORDER if kind.startswith("rotate")]
VTILES = 3
WINDOWS = (1, 3, 0, 2)


def before_in_slot(at, runs):
    mine = SLOT[PE_ORDER[at][:2]]
    for kind, n, back in reversed(PE_ORDER[:at]):
        if SLOT[kind, n] == mine and runs(back):
            return [(kind, n, back)]
    found = []
    if not runs(1):
        return found
    for kind, n, back in reversed(PE_ORDER):
        if SLOT[kind, n] == mine:
            found.append((kind, n, back + 1))
            if back == 0:
                break
    return found


def windowed_stack(nc, io, xT, ident):
    with ExitStack() as ctx:
        sb = lambda n, s, d=F32: ctx.enter_context(nc.sbuf_tensor(n, s, d))
        sem = lambda n: ctx.enter_context(nc.semaphore(n))
        w_qkv = sb("w_qkv", [P, 3, INNER])
        w_o = sb("w_o", [P, QCH, D])
        w_1 = sb("w_1", [P, 2, NJ, JW])
        w_2 = sb("w_2", [JW, NJ, D])
        b_1 = sb("b_1", [JW, 2, NJ])
        vec = sb("vec", [P, 3])
        qks = sb("qks", [P, 2, DH])
        rot = sb("rot", [P, TPB, 4, DH])
        table = sb("table", [P, TPB, 4, DH])
        ident16 = sb("ident16", [P, P], BF16)
        mask = sb("mask", [P, 2, SEQ], BF16)
        ones = sb("ones", [P, P])
        zero = sb("zero", [P, 1])
        epsc = sb("epsc", [P, 1])
        xs = sb("xs", [P, SEQ])
        sq = sb("sq", [P, 2, HEADS, DH])
        qk = sb("qk", [P, 2, HEADS, DH])
        mask32 = sq[:, 0].rearrange("p h d -> p (h d)").rearrange("p (a n) -> p a n", a=2)
        cosq = sb("cosq", [P, 2, HEADS, 2, DH // 2])
        sinq = sb("sinq", [P, 2, HEADS, 2, DH // 2])
        ss = sb("ss", [P, 2 * HEADS])
        half_ss = sb("half_ss", [P, 2 * HEADS])
        three_halves = sb("three_halves", [P, 2 * HEADS])
        ry = sb("ry", [P, 2 * HEADS])
        rt = sb("rt", [P, 2 * HEADS])
        rs = sb("rs", [P, 2 * HEADS])
        qT = sb("qT", [P, QCH, P])
        kT = [sb(f"kT{i}", [P, QCH, 2, WIN + P]) for i in range(2)]
        va = sb("va", [P, VTILES, 2, HEADS, VA])
        vb = sb("vb", [P, VTILES, 2, HEADS, VA])
        prob = sb("prob", [P, HEADS, DH])
        probT = sb("probT", [P, 8, P])
        smax = sb("smax", [P, HEADS])
        rden = sb("rden", [P, 2, 2, 4])
        o = sb("o", [P, 2, 4, 2, DH])
        oT = sb("oT", [P, QCH, SEQ])
        x1 = sb("x1", [P, SEQ])
        xs2 = sb("xs2", [P, SEQ])
        z = xs2
        xc = sb("xc", [P, SEQ])
        sqc = sb("sqc", [P, SEQ])
        gate = sqc[0:JW, :]
        hid = sb("hid", [JW, NJ, SEQ])
        slots = [ctx.enter_context(nc.psum_tensor(f"slot{i}", [P, 2, SEQ], F32)) for i in range(len(SLOTS_OF))]
        S = {n: sem("ws_" + n) for n in list(EVENTS) + ["const_loaded", "const_ready", "w_attn", "w_ff", "tables",
                                                        "cleared", "xs_ready", "norms_link", "s_link", "va_link", "vb_link", "ff_link", "pool_link", "passed"]}
        vb_ready = [sem(f"ws_vb_ready{t}") for t in range(TPB)]
        VB_DMAS = [3] + [4] * (TPB - 1)
        W_ATTN, W_FF = 2, 5
        CONSTS = 6
        block = ctx.enter_context(nc.Block())

        def passed(eng):
            eng.sem_inc(S["passed"], 1)

        def credit(eng, who):
            for name, (engine, n) in EVENTS.items():
                if engine == who:
                    eng.sem_inc(S[name], n)

        def wait(eng, name, unit, n=0):
            eng.wait_ge(S[name], (unit + 1) * EVENTS[name][1] + n + 1)

        def wait_tile(eng, name, unit, t, back=1):
            wait(eng, name, unit + (t - back) // TPB, (t - back) % TPB)

        def wait_vb(eng, unit, t):
            eng.wait_ge(vb_ready[t], 16 * VB_DMAS[t] * (unit + 2))

        def slot(kind, n=0):
            return slots[SLOT[kind, n]]

        def flat(kind, n=0):
            return slot(kind, n)[:, :, :].rearrange("p a n -> p (a n)")

        def units(eng, order, stage, layer_start=None, layer_end=None):
            def step(it, l, b, runs):
                starts = l if isinstance(b, int) and b == 0 else None
                if starts is not None and layer_start:
                    layer_start(it, l)
                for at, (kind, n, back) in enumerate(order):
                    if runs(back):
                        batch = b if back == 0 else (BATCH - 1 if starts is not None else b - 1)
                        stage(kind, n, it - back, batch, at, runs, starts)
                if starts is not None and layer_end:
                    layer_end(it, l)
            everything = lambda back: True
            step(0, 0, 0, lambda back: back == 0)
            with eng.Fori(1, BATCH) as b:
                step(b, 0, b, everything)
            with eng.Fori(1, DEPTH) as l:
                step(l * BATCH, l, 0, everything)
                with eng.Fori(1, BATCH) as b:
                    step(l * BATCH + b, l, b, everything)
            step(DEPTH * BATCH, None, BATCH, lambda back: back == 1)

        @block.sync
        def _(sp):
            for t in range(TPB):
                sp.sem_inc(vb_ready[t], 16 * VB_DMAS[t])
            sp.dma_start(rot[:, :, :, :], io["rot"]).then_inc(S["const_loaded"], 16)
            sp.dma_start(mask32, io["mask"]).then_inc(S["const_loaded"], 16)

            def load_ff(l):
                sp.dma_start(w_o[:, :, :], io["w_o"][l].rearrange("(c p) n -> p c n", p=P)).then_inc(S["w_ff"], 16)
                sp.dma_start(w_1[:, :, :, :].rearrange("p a j n -> p (a j n)"), io["w_1"][l]).then_inc(S["w_ff"], 16)
                sp.dma_start(w_2[:, :, :], io["w_2"][l].rearrange("(j p) n -> p j n", p=JW)).then_inc(S["w_ff"], 16)
                sp.dma_start(b_1[:, :, :].rearrange("p a j -> p (a j)"), io["b_1"][l]).then_inc(S["w_ff"], 16)
                sp.dma_start(vec[:, :], io["vec"][l]).then_inc(S["w_ff"], 16)

            def layer_start(it, l):
                kind, n = PROJECTIONS[-1]
                wait(sp, kind + "_filled", it - 1, n)
                passed(sp)
                sp.dma_start(w_qkv[:, :, :].rearrange("p a n -> p (a n)"), io["w_qkv"][l]).then_inc(S["w_attn"], 16)
                sp.dma_start(qks[:, :, :].rearrange("p a n -> p (a n)"), io["qk_scale"][l]).then_inc(S["w_attn"], 16)

            def layer_end(it, l):
                if not isinstance(l, int):
                    wait(sp, "y_read", it - 1)
                    load_ff(l)

            def stage(kind, t, unit, batch, at, runs, starts):
                s = t % VTILES
                wait(sp, "v_read", unit, t)
                sp.dma_start(vb[32:64, s, 0, :, :], va[0:32, s, 0, :, :]).then_inc(vb_ready[t], 16)
                sp.dma_start(vb[64:96, s, 1, :, :], va[32:64, s, 0, :, :]).then_inc(vb_ready[t], 16)
                sp.dma_start(vb[96:128, s, 1, :, :], va[64:96, s, 1, :, :]).then_inc(vb_ready[t], 16)
                if t:
                    sp.dma_start(vb[0:32, s, 0, :, :], va[96:128, (t - 1) % VTILES, 1, :, :]).then_inc(vb_ready[t], 16)
            load_ff(0)
            units(sp, SP_ORDER, stage, layer_start, layer_end)

        @block.gpsimd
        def _(pool):
            credit(pool, "pool")
            for v in (va, vb):
                pool.memset(v[:, :, :, :, :], 0.0).then_inc(S["cleared"], 1)
            for k in kT:
                pool.memset(k[:, :, :, :], 0.0).then_inc(S["cleared"], 1)
            for buffer, value in ((ones, 1.0 / D), (zero, 0.0), (epsc, EPS), (three_halves, 1.5), (xs, 0.0), (xs2, 0.0)):
                pool.memset(buffer[:, :], value).then_inc(S["cleared"], 1)
            pool.wait_ge(S["cleared"], 10)
            for v in (va, vb):
                pool.memset(v[0:DH, :, 0, :, DH:VA], 1.0).then_inc(S["const_ready"], 1)
                pool.memset(v[DH:P, :, 1, :, DH:VA], 1.0).then_inc(S["const_ready"], 1)
            STEPS = 3
            LINKS = 4 * STEPS - 1

            def stage(kind, t, unit, batch, at, runs, starts):
                if kind == "root":
                    wait(pool, "seeded", unit, t)
                    for k in range(STEPS):
                        for i, (dst, a, b, op) in enumerate(((rt, ry, ry, ALU.mult), (rt, rt, half_ss, ALU.mult),
                                                             (rt, rt, three_halves, ALU.add), (ry, ry, rt, ALU.mult))):
                            last = nc.gpsimd.tensor_tensor(dst[:, :], a[:, :], b[:, :], op)
                            if 4 * k + i < LINKS:
                                last.then_inc(S["pool_link"], 1)
                                pool.wait_ge(S["pool_link"], (unit * TPB + t) * LINKS + 4 * k + i + 1)
                    last.then_inc(S["rooted"], 1)
                else:
                    side = ("add_q", "add_k").index(kind)
                    wait(pool, "qk"[side] + "_read", unit, t)
                    nc.gpsimd.tensor_tensor(cosq[:, side], cosq[:, side], sinq[:, side], ALU.add).then_inc(
                        S["qk"[side] + "_added"], 1)
            units(pool, POOL_ORDER, stage)

        @block.vector
        def _(dve):
            credit(dve, "dve")
            dve.wait_ge(S["const_loaded"], 32)
            nc.vector.tensor_copy(mask[:, :, :], mask32).then_inc(S["const_ready"], 1)
            nc.vector.tensor_copy(ident16[:, :], ident[:, :]).then_inc(S["const_ready"], 1)
            dve.wait_ge(S["const_ready"], CONSTS)
            H = DH // 2
            LINKS = {"norms": 2, "s": 1, "va": 1, "vb": 1}

            def layer_tables(it, l):
                for name in "qk":
                    wait(dve, name + "_read", it - 1, TPB - 1)
                dve.wait_ge(S["w_attn"], 16 * W_ATTN * (l + 1))
                for side in range(2):
                    s = qks[:, side, :]
                    nc.vector.tensor_tensor(table[:, :, 2 * side, :], rot[:, :, 2 * side, :],
                                            s[:, None, :].broadcast_to([P, TPB, DH]), ALU.mult)
                    for half in range(2):
                        other = s[:, (1 - half) * H:(2 - half) * H]
                        last = nc.vector.tensor_tensor(
                            table[:, :, 2 * side + 1, half * H:half * H + H], rot[:, :, 2 * side + 1, half * H:half * H + H],
                            other[:, None, :].broadcast_to([P, TPB, H]), ALU.mult)
                last.then_inc(S["tables"], 1)
                dve.wait_ge(S["tables"], l + 1)
                passed(dve)

            def layer_end(it, l):
                dve.wait_ge(S["w_ff"], 16 * W_FF * (l + 1))
                passed(dve)

            def rotate(side, t, unit):
                name = "qk"[side]
                ps = flat(name, t).rearrange("p (h a d) -> p h a d", h=HEADS, a=2)
                cos, sin = table[:, t, 2 * side, :], table[:, t, 2 * side + 1, :]
                wait(dve, name + "_squared", unit, t)
                wait_tile(dve, name + "_scaled", unit, t)
                nc.vector.tensor_tensor(cosq[:, side].rearrange("p h a d -> p h (a d)"), ps.rearrange("p h a d -> p h (a d)"),
                                        cos[:, None, :].broadcast_to([P, HEADS, DH]), ALU.mult)
                for half in range(2):
                    last = nc.vector.tensor_tensor(
                        sinq[:, side, :, half, :], ps[:, :, 1 - half, :],
                        sin[:, None, half * H:half * H + H].broadcast_to([P, HEADS, H]), ALU.mult)
                last.then_inc(S[name + "_read"], 1)

            def stage(kind, n, unit, batch, at, runs, starts):
                def link(ins, name, i):
                    ins.then_inc(S[name + "_link"], 1)
                    dve.wait_ge(S[name + "_link"], (unit * TPB + n) * LINKS[name] + i + 1)

                if (kind, n) == ROTATIONS[0] and starts is not None:
                    layer_tables(unit, starts)
                if kind in ("rotate_q", "rotate_k"):
                    rotate(("rotate_q", "rotate_k").index(kind), n, unit)
                elif kind == "norms":
                    for name in "qk":
                        wait(dve, name + "_squared", unit, n)
                        wait_tile(dve, name + "_scaled", unit, n)
                    nc.vector.reduce_sum(ss[:, :], sq[:, :, :, :].rearrange("p a h d -> p (a h) d"), AX.X).then_inc(S["sumsq"], 1)
                    wait(dve, "sumsq", unit, n)
                    link(nc.vector.tensor_scalar(ss[:, :], ss[:, :], 1e-24, None, ALU.max), "norms", 0)
                    nc.vector.tensor_scalar(half_ss[:, :], ss[:, :], -0.5, None, ALU.mult)
                    link(nc.vector.tensor_single_scalar(rs[:, :].bitcast(I32), ss[:, :].bitcast(I32), 1, ALU.logical_shift_right),
                         "norms", 1)
                    nc.vector.tensor_scalar(ry[:, :].bitcast(I32), rs[:, :].bitcast(I32), -1.0, float(0x5F3759DF),
                                            ALU.mult, ALU.add).then_inc(S["seeded"], 1)
                elif kind in ("scale_q", "scale_k"):
                    side = ("scale_q", "scale_k").index(kind)
                    name = "qk"[side]
                    wait(dve, name + "_added", unit, n)
                    wait(dve, "rooted", unit, n)
                    wait_tile(dve, name + "T_filled", unit, n)
                    nc.vector.tensor_tensor(qk[:, side], cosq[:, side].rearrange("p h a d -> p h (a d)"),
                                            ry[:, side * HEADS:(side + 1) * HEADS, None].broadcast_to([P, HEADS, DH]),
                                            ALU.mult).then_inc(S[name + "_scaled"], 1)
                elif kind == "s":
                    wait(dve, "s_filled", unit, n)
                    wait_tile(dve, "r_filled", unit, n)
                    ps = flat("s", n).rearrange("p (s k) -> p s k", k=DH)
                    link(nc.vector.reduce_max(smax[:, :], ps, AX.X), "s", 0)
                    nc.vector.tensor_tensor(prob[:, :, :], ps, smax[:, :, None].broadcast_to([P, HEADS, DH]),
                                            ALU.subtract).then_inc(S["s_read"], 1)
                elif kind in ("va", "vb"):
                    a = ("va", "vb").index(kind)
                    wait(dve, kind + "_filled", unit, n)
                    wait_tile(dve, "o_filled", unit, n)
                    ps = slot(kind, n)[:, :, 0:4 * VA].rearrange("p r (w d) -> p r w d", d=VA)
                    link(nc.vector.reciprocal(rden[:, a], ps[:, :, :, DH]), kind, 0)
                    nc.vector.tensor_tensor(o[:, a].rearrange("p w r d -> p r w d"), ps[:, :, :, 0:DH],
                                            rden[:, a, :, :, None].broadcast_to([P, 2, 4, DH]), ALU.mult).then_inc(S[kind + "_read"], 1)
                elif kind == "residual":
                    wait(dve, "wo_filled", unit)
                    wait(dve, "y_read", unit - 1)
                    nc.vector.tensor_tensor(x1[:, :], slot("wo")[:, 0, :], xT[:, batch, :], ALU.add).then_inc(S["wo_read"], 1)
                elif kind == "center":
                    wait(dve, "mean_filled", unit)
                    nc.vector.tensor_tensor(xc[:, :], xs2[:, :], slot("mean")[:, 0, :], ALU.subtract).then_inc(S["mean_read"], 1)
                elif kind == "z":
                    wait(dve, "var_read", unit)
                    nc.vector.reciprocal(sqc[:, :], sqc[:, :]).then_inc(S["ff_link"], 1)
                    dve.wait_ge(S["ff_link"], 2 * unit + 1)
                    nc.vector.tensor_tensor(z[:, :], xc[:, :], sqc[:, :], ALU.mult).then_inc(S["ff_link"], 1)
                    dve.wait_ge(S["ff_link"], 2 * unit + 2)
                    nc.vector.tensor_scalar(z[:, :], z[:, :], vec[:, 0:1], vec[:, 1:2], ALU.mult, ALU.add).then_inc(S["z_ready"], 1)
                elif kind == "hid":
                    wait(dve, "gates", unit, n)
                    nc.vector.scalar_tensor_tensor(out=hid[:, n, :], in0=slot("h", n)[0:JW, 0, :], scalar=b_1[:, 0, n:n + 1],
                                                   in1=gate, op0=ALU.add, op1=ALU.mult).then_inc(S["h_read"], 1)
                elif kind == "y":
                    wait(dve, "y_filled", unit)
                    nc.vector.scalar_tensor_tensor(out=xT[:, batch, :], in0=slot("y")[:, 0, :], scalar=vec[:, 2:3],
                                                   in1=x1[:, :], op0=ALU.add, op1=ALU.add).then_inc(S["y_read"], 1)
            units(dve, DVE_ORDER, stage, None, layer_end)

        @block.scalar
        def _(act):
            credit(act, "act")
            act.wait_ge(S["const_ready"], CONSTS)

            def shift_tokens(dst, src, done):
                nc.scalar.copy(dst[0:DH, :], src[0:DH])
                nc.scalar.copy(dst[DH:P, 1:SEQ], src[DH:P, 0:SEQ - 1]).then_inc(done, 1)

            def layer_end(it, l):
                act.wait_ge(S["w_ff"], 16 * W_FF * (l + 1))
                passed(act)

            def stage(kind, n, unit, batch, at, runs, starts):
                if kind in ("square_q", "square_k"):
                    name = kind[-1]
                    wait(act, name + "_filled", unit, n)
                    wait_tile(act, "sumsq", unit, n)
                    nc.scalar.activation(sq[:, "qk".index(name)].rearrange("p h d -> p (h d)"), flat(name, n),
                                         ACT.Square).then_inc(S[name + "_squared"], 1)
                elif kind == "v":
                    old, unit_of = (0, unit) if n == VTILES else ((TPB - 1 if n == 0 else n), unit - 1)
                    wait(act, "vb_filled", unit_of, old)
                    wait_vb(act, unit_of, old)
                    if old + 1 < TPB:
                        wait_vb(act, unit_of, old + 1)
                    wait(act, "v_filled", unit, n)
                    ps = flat("v", n).rearrange("p (h d) -> p h d", d=DH)
                    nc.scalar.copy(va[0:DH, n % VTILES, 0, :, 0:DH], ps[0:DH])
                    nc.scalar.copy(va[DH:P, n % VTILES, 1, :, 0:DH], ps[DH:P]).then_inc(S["v_read"], 1)
                elif kind == "qT":
                    wait(act, "qT_filled", unit, n)
                    wait_tile(act, "s_filled", unit, n)
                    nc.scalar.copy(qT[:, :, :], flat("qT", n).rearrange("p (c n) -> p c n", n=P)).then_inc(S["qT_read"], 1)
                elif kind == "kT":
                    wait(act, "kT_filled", unit, n)
                    wait_tile(act, "s_filled", unit, n)
                    ps = flat("kT", n).rearrange("p (c n) -> p c n", n=P)
                    own, following = kT[n % 2], kT[(n + 1) % 2]
                    for r, rows in enumerate((slice(0, DH), slice(DH, P))):
                        nc.scalar.copy(own[rows, :, r, WIN:WIN + P], ps[rows])
                        last = nc.scalar.copy(following[rows, :, r, 0:WIN], ps[rows, :, P - WIN:P])
                    last.then_inc(S["kT_read"], 1)
                elif kind == "exp":
                    wait(act, "s_read", unit, n)
                    nc.scalar.activation(prob[:, :, :], prob[:, :, :], ACT.Exp).then_inc(S["probs"], 1)
                elif kind == "r":
                    wait(act, "r_filled", unit, n)
                    wait_tile(act, "vb_filled", unit, n)
                    nc.scalar.copy(probT[:, :, :], flat("r", n).rearrange("p (c n) -> p c n", n=P)).then_inc(S["r_read"], 1)
                elif kind == "o":
                    wait(act, "o_filled", unit, n)
                    wait(act, "wo_filled", unit - 1)
                    nc.scalar.copy(oT[:, :, n * P:(n + 1) * P].rearrange("p c (w n) -> p w c n", n=WIN),
                                   flat("o", n).rearrange("p (w c n) -> p w c n", w=4, n=WIN)).then_inc(S["o_read"], 1)
                elif kind == "next":
                    last_kind, last_n = PROJECTIONS[-1]
                    wait(act, last_kind + "_filled", unit, last_n)
                    shift_tokens(xs, xT[:, batch + 1 if isinstance(batch, int) else (batch + 1) % BATCH, :], S["xs_ready"])
                elif kind == "shift":
                    wait(act, "wo_read", unit)
                    wait(act, "h_filled", unit - 1, NJ - 1)
                    nc.scalar.mul(xs2[DH:P, 0:1], zero[DH:P, 0:1], 0.0)
                    shift_tokens(xs2, x1, S["xs2_ready"])
                elif kind == "square":
                    wait(act, "mean_read", unit)
                    nc.scalar.activation(sqc[:, :], xc[:, :], ACT.Square).then_inc(S["centered_sq"], 1)
                elif kind == "root":
                    wait(act, "var_filled", unit)
                    nc.scalar.activation(sqc[:, :], slot("var")[:, 0, :], ACT.Sqrt, bias=epsc[:, 0:1]).then_inc(S["var_read"], 1)
                elif kind == "gate":
                    if n:
                        wait(act, "h_read", unit, n - 1)
                    wait(act, "h_filled", unit, n)
                    nc.scalar.activation(gate, slot("h", n)[0:JW, 1, :], ACT.Gelu, bias=b_1[:, 1, n:n + 1]).then_inc(S["gates"], 1)
            shift_tokens(xs, xT[:, 0, :], S["xs_ready"])
            units(act, ACT_ORDER, stage, None, layer_end)

        @block.tensor
        def _(pe):
            credit(pe, "pe")
            pe.wait_ge(S["const_ready"], CONSTS)

            def layer_end(it, l):
                pe.wait_ge(S["w_ff"], 16 * W_FF * (l + 1))
                passed(pe)

            def transposes(kind, n, src, place=lambda c: c):
                for c in range(8):
                    k = place(c)
                    last = nc.tensor.transpose(flat(kind, n)[:, k * P:(k + 1) * P], src[:, c * P:(c + 1) * P], ident[:, :])
                return last

            def scores(t):
                for a in range(2):
                    nc.tensor.matmul(slot("s", t)[:, a, :], ident16[:, :], mask[:, 0 if t == 0 else 1, :],
                                     start=True, stop=False, skip_group_check=True)
                    for n, w in enumerate(WINDOWS):
                        tok = WIN * w
                        for g in range(4):
                            c = 4 * a + g
                            last = nc.tensor.matmul(
                                slot("s", t)[32 * g:32 * g + 32, a, :].rearrange("p (r k) -> p r k", r=2)[
                                    :, :, n * DH:(n + 1) * DH],
                                qT[:, c, tok:tok + WIN], kT[t % 2][:, c, :, tok:tok + 2 * WIN],
                                start=False, stop=True, skip_group_check=True)
                return last

            def products(kind, t):
                a = ("va", "vb").index(kind)
                for r in range(2):
                    for n, v in enumerate((va, vb)):
                        for g in range(4):
                            last = nc.tensor.matmul(
                                slot(kind, t)[32 * g:32 * g + 32, r, 2 * n * VA:2 * (n + 1) * VA],
                                probT[:, 4 * a + 2 * r + n, 32 * g:32 * g + 32],
                                v[:, t % VTILES, :, 2 * (4 * a + g) + r, :],
                                start=True, stop=True, skip_group_check=True)
                return last

            def stage(kind, n, unit, batch, at, runs, starts):
                back = PE_ORDER[at][2]
                for before, before_n, before_back in before_in_slot(at, runs):
                    wait(pe, before + "_read", unit + back - before_back, before_n)
                if kind in ("q", "k", "v"):
                    if (kind, n) == PROJECTIONS[0]:
                        pe.wait_ge(S["xs_ready"], unit + 1)
                        if starts is not None:
                            pe.wait_ge(S["w_attn"], 16 * W_ATTN * (starts + 1))
                            passed(pe)
                    for i in range(2):
                        last = nc.tensor.matmul(slot(kind, n)[:, i, :], xs[:, n * P:(n + 1) * P],
                                                w_qkv[:, "qkv".index(kind), i * SEQ:(i + 1) * SEQ], start=True, stop=True)
                elif kind in ("qT", "kT"):
                    wait(pe, kind[0] + "_scaled", unit, n)
                    last = transposes(kind, n, qk[:, "qk".index(kind[0])].rearrange("p h d -> p (h d)"))
                elif kind == "s":
                    wait(pe, "qT_read", unit, n)
                    wait(pe, "kT_read", unit, n)
                    last = scores(n)
                elif kind == "r":
                    wait(pe, "probs", unit, n)
                    last = transposes(kind, n, prob[:, :, :].rearrange("p h d -> p (h d)"))
                elif kind in ("va", "vb"):
                    if kind == "va":
                        wait(pe, "r_read", unit, n)
                        wait_vb(pe, unit, n)
                    passed(pe)
                    last = products(kind, n)
                elif kind == "o":
                    wait(pe, "va_read", unit, n)
                    wait(pe, "vb_read", unit, n)
                    last = transposes(kind, n, o[:, :, :, :, :].rearrange("p a w r d -> p (a w r d)"),
                                      lambda c: 2 * WINDOWS[c % 4] + c // 4)
                elif kind == "wo":
                    wait(pe, "o_read", unit, TPB - 1)
                    for c in range(QCH):
                        last = nc.tensor.matmul(slot("wo")[:, 0, :], w_o[:, c, :], oT[:, c, :], start=c == 0, stop=c == QCH - 1)
                elif kind == "mean":
                    wait(pe, "xs2_ready", unit)
                    last = nc.tensor.matmul(slot("mean")[:, 0, :], ones[:, :], xs2[:, :], start=True, stop=True)
                elif kind == "var":
                    wait(pe, "centered_sq", unit)
                    last = nc.tensor.matmul(slot("var")[:, 0, :], ones[:, :], sqc[:, :], start=True, stop=True)
                elif kind == "h":
                    wait(pe, "z_ready", unit)
                    for a in (1, 0):
                        last = nc.tensor.matmul(slot("h", n)[0:JW, a, :], w_1[:, a, n, :], z[:, :], start=True, stop=True)
                elif kind == "y":
                    wait(pe, "h_read", unit, NJ - 1)
                    for j in range(NJ):
                        last = nc.tensor.matmul(slot("y")[:, 0, :], w_2[:, j, :], hid[:, j, :], start=j == 0, stop=j == NJ - 1)
                last.then_inc(S[kind + "_filled"], 1)
            units(pe, PE_ORDER, stage, None, layer_end)


def add_up(nc, io, xT, ident):
    with ExitStack() as ctx:
        res = ctx.enter_context(nc.sbuf_tensor("fin_res", [P, TILES, D], F32))
        fetched = ctx.enter_context(nc.semaphore("fin_fetched"))
        sem = lambda n: ctx.enter_context(nc.semaphore(n))
        ps = [ctx.enter_context(nc.psum_tensor(f"fin_ps{i}", [P, 4 * P], F32)) for i in range(2)]
        turned, summed, stored = sem("fin_turned"), sem("fin_summed"), sem("fin_stored")
        block = ctx.enter_context(nc.Block())

        @block.tensor
        def _(pe):
            for b in range(BATCH):
                if b >= 2:
                    pe.wait_ge(summed, b - 1)
                for t in range(TPB):
                    last = nc.tensor.transpose(ps[b % 2][:, t * P:(t + 1) * P], xT[:, b, t * P:(t + 1) * P], ident[:, :])
                last.then_inc(turned, 1)

        @block.vector
        def _(dve):
            dve.wait_ge(fetched, 16)
            for b in range(BATCH):
                dve.wait_ge(turned, b + 1)
                r = res[:, TPB * b:TPB * (b + 1), :]
                nc.vector.tensor_tensor(r, r, ps[b % 2][:, :].rearrange("p (t d) -> p t d", d=D), ALU.add).then_inc(summed, 1)

        @block.sync
        def _(sp):
            sp.dma_start(res[:, :, :], io["kept"].rearrange("(n p) d -> p n d", p=P)).then_inc(fetched, 16)
            out = io["out"].rearrange("(n p) d -> p n d", p=P)
            for b in range(BATCH):
                sp.wait_ge(summed, b + 1)
                sp.dma_start(out[:, TPB * b:TPB * (b + 1), :], res[:, TPB * b:TPB * (b + 1), :]).then_inc(stored, 16)
            sp.wait_ge(stored, 16 * BATCH)


def build(nc, io):
    with nc.sbuf_tensor("xT", [P, BATCH, SEQ], F32) as xT, nc.sbuf_tensor("ident", [P, P], F32) as ident:
        with nc.sbuf_tensor("res", [P, TILES, D], F32) as res:
            layer_norm_and_transpose(nc, io, res, xT, ident)
            global_attention(nc, io, res, xT, ident)
        windowed_stack(nc, io, xT, ident)
        add_up(nc, io, xT, ident)


def rotation_tables():
    half = np.arange(0, DH, 2, dtype=np.float64)
    t = np.arange(SEQ, dtype=np.float64)
    freqs = t[:, None] * (1.0 / 10000.0 ** (half / DH))[None, :]
    scale = ((half + 0.4 * DH) / (1.4 * DH))[None, :] ** ((t - SEQ // 2) / (WIN // 2))[:, None]
    sign = np.concatenate([-np.ones(DH // 2), np.ones(DH // 2)])
    two = lambda a: np.concatenate([a, a], -1)
    cos, sin, scale = two(np.cos(freqs)), two(np.sin(freqs)) * sign, two(scale)
    kinds = np.stack([8.0 * cos * scale, 8.0 * sin * scale, cos / scale, sin / scale], 1)
    return np.ascontiguousarray(kinds.reshape(TPB, P, 4, DH).transpose(1, 0, 2, 3).astype(np.float32))


def window_masks():
    i = np.arange(P)[:, None] % WIN
    j = np.arange(2 * WIN)[None, :]
    block = np.where((j >= i) & (j <= i + WIN), 0.0, MASKED)
    first = np.where((j >= WIN) & (j <= i + WIN), 0.0, MASKED)
    rows = lambda w0: np.tile(np.concatenate([block, block, w0, block], 1), (1, 2))
    return np.ascontiguousarray(np.stack([rows(first), rows(block)], 1).astype(np.float32))


def kernel(**inputs):
    import concourse.bacc as bacc
    from concourse.bass_utils import run_bass_kernel_spmd

    f = {k[3:]: np.asarray(v) for k, v in inputs.items()}
    w = f["attn_Wqkv"].reshape(CH, 3, HD, D).transpose(3, 1, 0, 2).reshape(D, 3 * D)
    bq = f["attn_bqkv"].reshape(CH, 3, HD).transpose(1, 0, 2).reshape(1, 3 * D)
    w1 = np.zeros((DEPTH, D, 2, NJ * JW), np.float32)
    w1[:, :, :, :DIN] = f["ffn_W1"].reshape(DEPTH, D, 2, DIN)
    b1 = np.zeros((DEPTH, 2, NJ * JW), np.float32)
    b1[:, :, :DIN] = f["ffn_b1"].reshape(DEPTH, 2, DIN)
    w2 = np.zeros((DEPTH, NJ * JW, D), np.float32)
    w2[:, :DIN] = f["ffn_W2"]
    scales = np.concatenate([f["ffn_q_scale"], f["ffn_k_scale"]], 1)[:, None, :]
    arrays = {
        "x": f["attn_x"].reshape(TOKENS, D),
        "ident": np.eye(P, dtype=np.float32),
        "bo_rows": np.broadcast_to(f["attn_bo"], (P, D)),
        "at_wqkvT": w,
        "at_woT": f["attn_Wo"].T,
        "at_bias": np.broadcast_to(bq, (P, 3 * D)),
        "rot": rotation_tables(),
        "mask": window_masks(),
        "w_qkv": f["ffn_Wqkv"],
        "qk_scale": np.broadcast_to(scales, (DEPTH, P, 2 * DH)),
        "w_o": f["ffn_Wo"],
        "w_1": w1.reshape(DEPTH, D, 2 * NJ * JW),
        "w_2": w2,
        "b_1": b1.reshape(DEPTH, 2, NJ, JW).transpose(0, 3, 1, 2).reshape(DEPTH, JW, 2 * NJ),
        "vec": np.stack([f["ffn_ln_g"], f["ffn_ln_b"], f["ffn_b2"]], 2),
    }
    arrays = {f"in_{k}": np.ascontiguousarray(v) for k, v in arrays.items()}
    nc = bacc.Bacc("TRN2", target_bir_lowering=False, num_devices=1)
    io = {k[3:]: nc.dram_tensor(k, v.shape, F32, kind="ExternalInput").ap() for k, v in arrays.items()}
    io["out"] = nc.dram_tensor("out_0", (TOKENS, D), F32, kind="ExternalOutput").ap()
    io["kept"] = nc.dram_tensor("kept", (TOKENS, D), F32, kind="Internal").ap()
    build(nc, io)
    r = run_bass_kernel_spmd(nc, [arrays], core_ids=[0])
    return r.results[0]["out_0"].reshape(BATCH, SEQ, D)
```

```python
import numpy as np
import concourse.bass as bass
from concourse import mybir
from contextlib import ExitStack

F32 = mybir.dt.float32
BF16 = mybir.dt.bfloat16
I32 = mybir.dt.int32
ALU = mybir.AluOpType
ACT = mybir.ActivationFunctionType
AX = mybir.AxisListType

P = 128
D = 128
BATCH, SEQ = 8, 512
TOKENS = BATCH * SEQ
TILES = TOKENS // P
HEADS = 16

HD = D // HEADS
CH = SEQ // 32
HPT = P // 32
SLOTS = 64
SHIFT_ROW = 6 * HD

DEPTH, DH, WIN = 6, 64, 32
INNER = HEADS * DH
QCH = INNER // P
DIN = int(D * 4 * 2 / 3)
NJ = 3
JW = (DIN + NJ - 1) // NJ
TPB = SEQ // P
EPS = 1e-5
MASKED = -1.0e30
VA = DH + 1


def layer_norm_and_transpose(nc, io, res, xT, ident):
    with ExitStack() as ctx:
        sb = lambda n, s, d=F32: ctx.enter_context(nc.sbuf_tensor(n, s, d))
        sem = lambda n: ctx.enter_context(nc.semaphore(n))
        xn = sb("ln_xn", [P, TILES, D])
        stats = sb("ln_stats", [P, TILES, 6])
        agg = sb("ln_agg", [P, TILES, 2])
        std = sb("ln_std", [P, TILES])
        rstd = sb("ln_rstd", [P, TILES])
        bo = sb("ln_bo", [P, D])
        ps = [ctx.enter_context(nc.psum_tensor(f"ln_ps{i}", [P, 4 * P], F32)) for i in range(2)]
        loaded, stats_done, agg_done, std_done, rstd_done, xn_done, moved, transposed = map(
            sem, ("ln_loaded", "ln_stats_done", "ln_agg_done", "ln_std_done", "ln_rstd_done", "ln_xn_done",
                  "ln_moved", "ln_transposed"))
        PART = TILES // 4
        x_loaded = [sem(f"ln_x_loaded{c}") for c in range(4)]
        block = ctx.enter_context(nc.Block())

        @block.sync
        def _(sp):
            x = io["x"].rearrange("(n p) d -> p n d", p=P)
            for c, done in enumerate(x_loaded):
                sp.dma_start(res[:, c * PART:(c + 1) * PART, :], x[:, c * PART:(c + 1) * PART, :]).then_inc(done, 16)
            sp.dma_start(ident[:, :], io["ident"]).then_inc(loaded, 16)
            sp.dma_start(bo[:, :], io["bo_rows"]).then_inc(loaded, 16)

        @block.vector
        def _(dve):
            for i in range(TILES):
                if i % PART == 0:
                    dve.wait_ge(x_loaded[i // PART], 16)
                nc.vector.bn_stats(stats[:, i, :], res[:, i, :]).then_inc(stats_done, 1)
            for i in range(TILES):
                dve.wait_ge(stats_done, i + 1)
                nc.vector.bn_aggr(agg[:, i, :], stats[:, i, :]).then_inc(agg_done, 1)
            dve.wait_ge(agg_done, TILES)
            nc.vector.tensor_scalar(std[:, :], agg[:, :, 1], EPS, None, ALU.add).then_inc(agg_done, 1)
            dve.wait_ge(std_done, 1)
            nc.vector.reciprocal(rstd[:, :], std[:, :]).then_inc(rstd_done, 1)
            dve.wait_ge(rstd_done, 1)
            for i in range(TILES):
                nc.vector.tensor_scalar(xn[:, i, :], res[:, i, :], agg[:, i, 0:1], rstd[:, i:i + 1],
                                        ALU.subtract, ALU.mult).then_inc(xn_done, 1)
            dve.wait_ge(xn_done, TILES)
            dve.wait_ge(loaded, 32)
            nc.vector.tensor_tensor(res[:, :, :], res[:, :, :],
                                    bo[:, None, :].broadcast_to([P, TILES, D]), ALU.add).then_inc(xn_done, 1)

        @block.scalar
        def _(act):
            act.wait_ge(agg_done, TILES + 1)
            nc.scalar.activation(std[:, :], std[:, :], ACT.Sqrt).then_inc(std_done, 1)
            for b in range(BATCH):
                act.wait_ge(transposed, b + 1)
                nc.scalar.copy(xT[:, b, :], ps[b % 2][:, :]).then_inc(moved, 1)

        @block.tensor
        def _(pe):
            pe.wait_ge(loaded, 32)
            for b in range(BATCH):
                pe.wait_ge(xn_done, TPB * (b + 1))
                if b >= 2:
                    pe.wait_ge(moved, b - 1)
                for t in range(TPB):
                    last = nc.tensor.transpose(ps[b % 2][:, t * P:(t + 1) * P], xn[:, TPB * b + t, :], ident[:, :])
                last.then_inc(transposed, 1)


def stages(text):
    out = []
    for word in text.split():
        name = word.rstrip("-")
        kind = name.rstrip("0123456789")
        out.append((kind, int(name[len(kind):] or 0), len(word) - len(name)))
    return out


CREDIT = 2


def credit(eng, S, events, who):
    for name, (engine, n) in events.items():
        if engine == who:
            eng.sem_inc(S[name], CREDIT * n)


def event_wait(S, events):
    def wait(eng, name, unit, n=0):
        eng.wait_ge(S[name], (unit + CREDIT) * events[name][1] + n + 1)
    return wait


def forerunners(order, slot_of, at, step, looped, count):
    found = []
    for ago in range(min(step, 2) + 1):
        for kind, n, back in reversed(order[:at] if ago == 0 else order):
            unit = step - ago - back
            if slot_of.get((kind, n)) != slot_of[order[at][:2]]:
                continue
            if looped:
                found.append((kind, n, back + ago))
                if unit >= 0:
                    return found
            elif 0 <= unit < count:
                return [(kind, n, back + ago)]
    return found



AT_PE_ORDER = stages(
    "stack3- proj scores0-- max0- max1- max2- scores1-- scores2-- max3- max4- scores3-- max5- scores4-- max6- "
    "max7- scores5-- max8- max9- pv0-- max10- max11- scores6-- max12- scores7-- max13- max14- stack0 max15- "
    "pv1-- shift- stack1 stack2 vals-- y-- ")
AT_DVE_ORDER = stages(
    "bias max0- max1- max2- max3- max4- max5- max6- max7- max8- max9- max10- max11- max12- max13- max14- "
    "max15- shift- outputs-- values result-- ")
AT_ACT_ORDER = stages(
    "take stack2- stack3- exp0-- exp1-- exp2-- exp3-- exp4-- exp5-- exp6-- exp7-- stack0 shift- stack1 vals-- ")
AT_POOL_ORDER = stages(
    "parts place ")
AT_SP_ORDER = stages(
    "dma- ")

AT_SLOTS_OF = (
    "proj stack1 max2 max4 max6 max9 max11 max14 y ",
    "stack2 max1 max3 max5 max8 max10 max13 max15 shift ",
    "stack0 stack3 max0 max7 max12 vals ",
    "scores0 scores2 scores4 scores7 ",
    "scores1 scores3 scores5 scores6 ",)

AT_FILLS = {"proj": (1, "dve"), "stack": (4, "act"), "max": (16, "dve"), "shift": (1, "act"), "scores": (8, "act"),
            "vals": (1, "act"), "y": (1, "dve")}
AT_EVENTS = {"x_taken": ("act", 1), "parted": ("pool", 1), "v_placed": ("dve", 1), "stacked": ("pool", 1),
             "shift_parted": ("dve", 1), "pv_done": ("pe", 2), "o_taken": ("dve", 1), "vals_done": ("dve", 1)}
AT_EVENTS.update({kind + "_filled": ("pe", n) for kind, (n, _) in AT_FILLS.items()})
AT_EVENTS.update({kind + "_read": (engine, n) for kind, (n, engine) in AT_FILLS.items()})
AT_SLOT = {(kind, n): k for k, names in enumerate(AT_SLOTS_OF) for kind, n, _ in stages(names)}


def global_attention(nc, io, res, xT, ident):
    with ExitStack() as ctx:
        sb = lambda n, s, d=F32: ctx.enter_context(nc.sbuf_tensor(n, s, d))
        sem = lambda n: ctx.enter_context(nc.semaphore(n))
        w_qkv = sb("at_wqkv", [P, 3 * P])
        w_o = sb("at_wo", [P, P])
        bias = sb("at_bias", [P, 3 * P])
        ident16 = sb("at_ident16", [P, P], BF16)
        xg = sb("at_xg", [P, P])
        qkv = sb("at_qkv", [P, 3, CH, HD])
        part = sb("at_part", [P, 3, 2, CH, HD], BF16)
        rest = sb("at_rest", [P, 2, CH, HD])
        stack = sb("at_stack", [P, 2, CH, SLOTS], BF16)
        qs = [sb(f"at_qs{i}", [P, HPT, CH, 32], BF16) for i in range(2)]
        ks = [sb(f"at_ks{i}", [P, HPT, CH, 32], BF16) for i in range(2)]
        vs = [sb(f"at_vs{i}", [P, HPT, 4, 32]) for i in range(2)]
        rowmax = sb("at_rowmax", [P, HPT * 4])
        mrest = sb("at_mrest", [P, HPT * 4])
        mpart = sb("at_mpart", [P, 3, HPT * 4], BF16)
        mT = sb("at_mT", [3 * HPT * 4, P], BF16)
        probs = [sb(f"at_probs{i}", [P, 2, SEQ]) for i in range(2 * HPT)]
        oT = sb("at_oT", [P, CH, 32])
        rden = sb("at_rden", [P, CH])
        vals = sb("at_vals", [P, CH, HD])
        valsT = sb("at_valsT", [P, P])
        slots = [ctx.enter_context(nc.psum_tensor(f"at_slot{i}", [P, SEQ] if i < 3 else [P, 2, SEQ], F32)) for i in range(5)]
        ps_o = ctx.enter_context(nc.psum_tensor("at_po", [P, SEQ], F32))
        S = {n: sem("at_" + n) for n in list(AT_EVENTS) + [
            "loaded", "cleared", "ident_done", "biased", "parts_link", "shift_link", "outputs_link", "shift_rows",
            "passed", "kept"]}
        block = ctx.enter_context(nc.Block())
        SCALE = 1.0 / float(np.sqrt(HD))
        wait = event_wait(S, AT_EVENTS)

        def passed(eng):
            eng.sem_inc(S["passed"], 1)

        def slot(kind, n=0):
            return slots[AT_SLOT[kind, n]]

        def units(eng, order, stage):
            def step(s, first, looped):
                for at, (kind, n, back) in enumerate(order):
                    if looped or 0 <= first - back < TILES:
                        before = []
                        if order is AT_PE_ORDER and (kind, n) in AT_SLOT:
                            before = [(k, m, s - ago) for k, m, ago in
                                      forerunners(order, AT_SLOT, at, first, looped, TILES)]
                        stage(kind, n, s - back, (first - back) % 2, before)
            for s in range(2):
                step(s, s, False)
            with eng.Fori(1, TILES // 2) as i:
                step(2 * i, 2, True)
                step(2 * i + 1, 3, True)
            for s in range(TILES, TILES + 2):
                step(s, s, False)

        @block.sync
        def _(sp):
            sp.dma_start(w_qkv[:, :], io["at_wqkvT"]).then_inc(S["loaded"], 16)
            sp.dma_start(w_o[:, :], io["at_woT"]).then_inc(S["loaded"], 16)
            sp.dma_start(bias[:, :], io["at_bias"]).then_inc(S["loaded"], 16)

            def stage(kind, n, g, par, before):
                wait(sp, "shift_read", g)
                sp.dma_start(qs[par][SHIFT_ROW:SHIFT_ROW + 3, :, :, :].rearrange("p h c t -> p (h c t)")
                             .rearrange("p (r q) -> p r q", q=P),
                             mT[:, :]).then_inc(S["shift_rows"], 16)
            units(sp, AT_SP_ORDER, stage)
            wait(sp, "y_read", TILES - 1)
            sp.dma_start(io["kept"].rearrange("(n p) d -> p n d", p=P), res[:, :, :]).then_inc(S["kept"], 16)
            sp.wait_ge(S["kept"], 16)

        @block.gpsimd
        def _(pool):
            credit(pool, S, AT_EVENTS, "pool")
            pool.memset(stack[:, :, :, :], 0.0).then_inc(S["cleared"], 1)
            pool.wait_ge(S["cleared"], 1)
            pool.memset(stack[:, 1, :, SHIFT_ROW:SHIFT_ROW + 3], 1.0).then_inc(S["cleared"], 1)
            for buffers in (ks, qs):
                for buffer in buffers:
                    pool.memset(buffer[:, :, :, :], 0.0).then_inc(S["cleared"], 1)
            for v in vs:
                pool.memset(v[:, :, :, :], 0.0).then_inc(S["cleared"], 1)
            pool.wait_ge(S["cleared"], 8)
            for v in vs:
                pool.memset(v[:, :, :, HD:HD + 1], 1.0).then_inc(S["cleared"], 1)
            pool.wait_ge(S["cleared"], 10)

            def copy(dst, src):
                return nc.gpsimd.tensor_scalar(dst, src, 1.0, 0.0, ALU.mult, ALU.add)

            LINKS = 3

            def link(ins, g, i):
                ins.then_inc(S["parts_link"], 1)
                pool.wait_ge(S["parts_link"], g * LINKS + i)

            def stage(kind, n, g, par, before):
                if kind == "parts":
                    pool.wait_ge(S["biased"], g + 1)
                    wait(pool, "stacked", g - 1)
                    passed(pool)
                    link(copy(part[:, 0], qkv[:, 0:2]), g, 1)
                    link(nc.gpsimd.tensor_tensor(rest[:, :], qkv[:, 0:2], part[:, 0], ALU.subtract), g, 2)
                    passed(pool)
                    link(copy(part[:, 1], rest[:, :]), g, 3)
                    nc.gpsimd.tensor_tensor(part[:, 2], rest[:, :], part[:, 1], ALU.subtract).then_inc(S["parted"], 1)
                else:
                    wait(pool, "parted", g)
                    wait(pool, "stack_filled", g - 1, 3)
                    passed(pool)
                    for side, row, p in ((0, 0, 0), (0, 1, 0), (0, 2, 1), (0, 3, 0), (0, 4, 1), (0, 5, 2),
                                         (1, 0, 0), (1, 1, 1), (1, 2, 0), (1, 3, 2), (1, 4, 1), (1, 5, 0)):
                        last = copy(stack[:, side, :, row * HD:(row + 1) * HD], part[:, p, side, :, :])
                    last.then_inc(S["stacked"], 1)
            units(pool, AT_POOL_ORDER, stage)

        @block.vector
        def _(dve):
            credit(dve, S, AT_EVENTS, "dve")
            dve.wait_ge(S["loaded"], 48)
            nc.vector.tensor_copy(ident16[:, :], ident[:, :]).then_inc(S["ident_done"], 1)
            dve.wait_ge(S["cleared"], 10)
            LINKS = {"shift": 5, "outputs": 1}

            def stage(kind, n, g, par, before):
                links = [0]

                def link(ins):
                    links[0] += 1
                    ins.then_inc(S[kind + "_link"], 1)
                    dve.wait_ge(S[kind + "_link"], g * LINKS[kind] + links[0])

                if kind == "bias":
                    wait(dve, "proj_filled", g)
                    wait(dve, "parted", g - 1)
                    wait(dve, "v_placed", g - 1)
                    nc.vector.tensor_tensor(qkv[:, :, :, :].rearrange("p a c d -> p (a c d)"), slot("proj")[:, 0:3 * P],
                                            bias[:, :], ALU.add).then_inc(S["proj_read"], 1)
                    wait(dve, "proj_read", g)
                    dve.sem_inc(S["biased"], 1)
                elif kind == "values":
                    wait(dve, "proj_read", g)
                    wait(dve, "pv_done", g - 2, 1)
                    for h in range(HPT):
                        for c4 in range(4):
                            last = nc.vector.tensor_copy(
                                vs[par][32 * c4:32 * c4 + 32, h, :, 0:HD],
                                qkv[32 * h:32 * h + 32, 2, :, :].rearrange("p (b c) d -> p b c d", c=4)[:, :, c4, :])
                    last.then_inc(S["v_placed"], 1)
                elif kind == "max":
                    wait(dve, "max_filled", g, n)
                    if n == 0:
                        wait(dve, "shift_parted", g - 1)
                    nc.vector.reduce_max(rowmax[:, n:n + 1], slot("max", n)[:, :], AX.X).then_inc(S["max_read"], 1)
                elif kind == "shift":
                    wait(dve, "max_read", g, 15)
                    wait(dve, "shift_filled", g - 1)
                    link(nc.vector.tensor_scalar(mrest[:, :], rowmax[:, :], -1.0, None, ALU.mult))
                    link(nc.vector.tensor_copy(mpart[:, 0, :], mrest[:, :]))
                    link(nc.vector.tensor_tensor(mrest[:, :], mrest[:, :], mpart[:, 0, :], ALU.subtract))
                    link(nc.vector.tensor_copy(mpart[:, 1, :], mrest[:, :]))
                    link(nc.vector.tensor_tensor(mrest[:, :], mrest[:, :], mpart[:, 1, :], ALU.subtract))
                    nc.vector.tensor_copy(mpart[:, 2, :], mrest[:, :]).then_inc(S["shift_parted"], 1)
                elif kind == "outputs":
                    wait(dve, "pv_done", g, 1)
                    wait(dve, "vals_filled", g - 1)
                    nc.vector.transpose(oT[:, :, :].rearrange("p c d -> p (c d)"), ps_o[:, :]).then_inc(S["o_taken"], 1)
                    wait(dve, "o_taken", g)
                    link(nc.vector.reciprocal(rden[:, :], oT[:, :, HD]))
                    nc.vector.tensor_tensor(vals[:, :, :], oT[:, :, 0:HD], rden[:, :, None].broadcast_to([P, CH, HD]),
                                            ALU.mult).then_inc(S["vals_done"], 1)
                else:
                    wait(dve, "y_filled", g)
                    nc.vector.tensor_tensor(res[:, g, :], res[:, g, :], slot("y")[:, 0:P], ALU.add).then_inc(S["y_read"], 1)
            units(dve, AT_DVE_ORDER, stage)

        @block.scalar
        def _(act):
            credit(act, S, AT_EVENTS, "act")
            act.wait_ge(S["cleared"], 10)

            def stage(kind, n, g, par, before):
                if kind == "take":
                    wait(act, "proj_filled", g - 1)
                    nc.scalar.copy(xg[:, :], xT[:, :, :].rearrange("p b s -> p (b s)")[:, bass.ts(g, P)]).then_inc(S["x_taken"], 1)
                elif kind == "stack":
                    side, half = n // 2, n % 2
                    wait(act, "stack_filled", g, n)
                    wait(act, "scores_filled", g - 2, 7)
                    dst = (qs, ks)[side][par][0:SLOTS, :, half * 8:half * 8 + 8, :].rearrange("p h c t -> p c h t")
                    src = slot("stack", n)[:, :].bitcast(BF16)[0:SLOTS, :].rearrange("p (c h t) -> p c h t", h=HPT, t=32)
                    nc.scalar.copy(dst, src).then_inc(S["stack_read"], 1)
                elif kind == "shift":
                    wait(act, "shift_filled", g)
                    act.wait_ge(S["shift_rows"], 16 * g)
                    nc.scalar.copy(mT[:, :], slot("shift")[:, 0:P // 2].bitcast(BF16)[0:3 * HPT * 4, :]).then_inc(S["shift_read"], 1)
                elif kind == "exp":
                    wait(act, "scores_filled", g, n)
                    wait(act, "pv_done", g - 1, n // HPT)
                    nc.scalar.activation(probs[n][:, :, :], slot("scores", n)[:, :, :], ACT.Exp,
                                         scale=SCALE).then_inc(S["scores_read"], 1)
                else:
                    wait(act, "vals_filled", g)
                    wait(act, "y_filled", g - 1)
                    nc.scalar.copy(valsT[:, :], slot("vals")[:, 0:P]).then_inc(S["vals_read"], 1)
            units(act, AT_ACT_ORDER, stage)

        @block.tensor
        def _(pe):
            credit(pe, S, AT_EVENTS, "pe")
            pe.wait_ge(S["ident_done"], 1)
            pe.wait_ge(S["cleared"], 10)

            def stage(kind, n, g, par, before):
                for filled, m, unit in before:
                    wait(pe, filled + "_read", unit, m)
                done = S[kind + "_filled"] if kind != "pv" else S["pv_done"]
                if kind == "proj":
                    wait(pe, "x_taken", g)
                    last = nc.tensor.matmul(slot("proj")[:, 0:3 * P], xg[:, :], w_qkv[:, :], start=True, stop=True)
                elif kind == "stack":
                    side, half = n // 2, n % 2
                    wait(pe, "stacked", g)
                    passed(pe)
                    for c in range(8):
                        last = nc.tensor.transpose(slot("stack", n)[:, :].bitcast(BF16)[0:SLOTS, c * P:(c + 1) * P],
                                                   stack[:, side, 8 * half + c, :], ident16[:, :])
                elif kind == "max":
                    h, qc = n // 4, n % 4
                    if n == 0:
                        wait(pe, "stack_read", g, 3)
                    last = nc.tensor.matmul(slot("max", n)[:, :],
                                            qs[par][:, h, :, :].rearrange("p c t -> p (c t)")[:, qc * P:(qc + 1) * P],
                                            ks[par][:, h, :, :].rearrange("p c t -> p (c t)"), start=True, stop=True)
                elif kind == "shift":
                    wait(pe, "shift_parted", g)
                    passed(pe)
                    last = nc.tensor.transpose(slot("shift")[:, 0:P // 2].bitcast(BF16)[0:3 * HPT * 4, :],
                                               mpart[:, :, :].rearrange("p a b -> p (a b)"), ident16[:, :])
                elif kind == "scores":
                    h, pair = n % HPT, n // HPT
                    if n == 0:
                        pe.wait_ge(S["shift_rows"], 16 * g + 16)
                    for i in range(2):
                        kc = 2 * pair + i
                        last = nc.tensor.matmul(
                            slot("scores", n)[:, i, :],
                            ks[par][:, h, :, :].rearrange("p c t -> p (c t)")[:, kc * P:(kc + 1) * P],
                            qs[par][:, h, :, :].rearrange("p c t -> p (c t)"), start=True, stop=True)
                elif kind == "pv":
                    if n == 0:
                        wait(pe, "v_placed", g)
                        wait(pe, "o_taken", g - 1)
                    wait(pe, "scores_read", g, n * HPT + HPT - 1)
                    for i in range(2):
                        kc = 2 * n + i
                        for h in range(HPT):
                            last = nc.tensor.matmul(ps_o[32 * h:32 * h + 32, :], vs[par][:, h, kc, :],
                                                    probs[n * HPT + h][:, i, :], start=kc == 0, stop=kc == 3)
                elif kind == "vals":
                    wait(pe, "vals_done", g)
                    last = nc.tensor.transpose(slot("vals")[:, 0:P], vals[:, :, :].rearrange("p c d -> p (c d)"), ident[:, :])
                else:
                    wait(pe, "vals_read", g)
                    last = nc.tensor.matmul(slot("y")[:, 0:P], valsT[:, :], w_o[:, :], start=True, stop=True)
                last.then_inc(done, 1)
            units(pe, AT_PE_ORDER, stage)


PE_ORDER = stages(
    "o0- r1- s2- q0 kT3- va1- k0 vb1- qT3- r2- o1- s3- va2- vb2- q1 r3- k1 o2- qT0 va3- vb3- kT0 k2 o3- s0 wo- q2 "
    "v0 mean- qT1 r0 var- v1 kT1 k3 va0 s1 h0- h1- h2- vb0 q3 v2 qT2 y- kT2 v3 ")
DVE_ORDER = stages(
    "scale_k3- scale_q3- s2- rotate_q0 va1- vb1- norms0 rotate_k0 s3- va2- vb2- scale_q0 rotate_q1 scale_k0 va3- "
    "vb3- norms1 rotate_k1 s0 scale_q1 scale_k1 rotate_k2 residual- center- rotate_q2 norms2 z- va0 s1 scale_q2 hid0- "
    "scale_k2 hid1- vb0 hid2- rotate_k3 norms3 rotate_q3 y- ")
ACT_ORDER = stages(
    "o0- r1- v3- square_q0 kT3- square_k0 exp2- qT3- r2- o1- exp3- square_q1 r3- o2- qT0 square_k1 kT0 o3- "
    "square_k2 exp0 shift- square_q2 v0 square- qT1 r0 root- kT1 v1 gate0- square_k3 gate1- gate2- exp1 square_q3 "
    "v2 qT2 kT2 next ")
POOL_ORDER = stages(
    "add_k3- root3- add_q3- add_q0 root0 add_k0 add_q1 root1 add_k1 add_q2 root2 add_k2 ")
SP_ORDER = stages(
    "vb2- vb3- vb0 vb1 ")

SLOTS_OF = (
    "qT0 vb0 v1 qT1 k2 v2 v3 qT3 kT3 s3 r3 h0",
    "k0 kT0 s0 q1 kT1 s1 q2 qT2 kT2 s2 va3 h2",
    "va0 o0 va1 o1 va2 o2 q3 vb3 o3 wo mean var h1",
    "q0 v0 r0 k1 r1 vb1 r2 vb2 k3 y",)

FILLS = {"q": (TPB, "dve"), "k": (TPB, "dve"), "v": (TPB, "act"), "qT": (TPB, "act"), "kT": (TPB, "act"),
         "s": (TPB, "dve"), "r": (TPB, "act"), "va": (TPB, "dve"), "vb": (TPB, "dve"), "o": (TPB, "act"),
         "wo": (1, "dve"), "mean": (1, "dve"), "var": (1, "act"), "h": (NJ, "dve"), "y": (1, "dve")}
EVENTS = {"q_squared": ("act", TPB), "k_squared": ("act", TPB), "sumsq": ("dve", TPB), "seeded": ("dve", TPB),
          "q_added": ("pool", TPB), "k_added": ("pool", TPB), "rooted": ("pool", TPB),
          "q_scaled": ("dve", TPB), "k_scaled": ("dve", TPB), "probs": ("act", TPB),
          "xs2_ready": ("act", 1), "centered_sq": ("act", 1), "z_ready": ("dve", 1), "gates": ("act", NJ)}
EVENTS.update({kind + "_filled": ("pe", n) for kind, (n, _) in FILLS.items()})
EVENTS.update({kind + "_read": (engine, n) for kind, (n, engine) in FILLS.items()})
SLOT = {(kind, n): k for k, names in enumerate(SLOTS_OF) for kind, n, _ in stages(names)}
PROJECTIONS = [(kind, n) for kind, n, _ in PE_ORDER if kind in ("q", "k", "v")]
ROTATIONS = [(kind, n) for kind, n, _ in DVE_ORDER if kind.startswith("rotate")]
VTILES = 3
WINDOWS = (1, 3, 0, 2)


def windowed_stack(nc, io, xT, ident):
    with ExitStack() as ctx:
        sb = lambda n, s, d=F32: ctx.enter_context(nc.sbuf_tensor(n, s, d))
        sem = lambda n: ctx.enter_context(nc.semaphore(n))
        w_qkv = sb("w_qkv", [P, 3, INNER])
        w_o = sb("w_o", [P, QCH, D])
        w_1 = sb("w_1", [P, 2, NJ, JW])
        w_2 = sb("w_2", [JW, NJ, D])
        b_1 = sb("b_1", [JW, 2, NJ])
        vec = sb("vec", [P, 3])
        qks = sb("qks", [P, 2, DH])
        rot = sb("rot", [P, TPB, 4, DH])
        table = sb("table", [P, TPB, 4, DH])
        ident16 = sb("ident16", [P, P], BF16)
        mask = sb("mask", [P, 2, SEQ], BF16)
        ones = sb("ones", [P, P])
        zero = sb("zero", [P, 1])
        epsc = sb("epsc", [P, 1])
        xs = sb("xs", [P, SEQ])
        sq = sb("sq", [P, 2, HEADS, DH])
        qk = sb("qk", [P, 2, HEADS, DH])
        mask32 = sq[:, 0].rearrange("p h d -> p (h d)").rearrange("p (a n) -> p a n", a=2)
        cosq = sb("cosq", [P, 2, HEADS, 2, DH // 2])
        sinq = sb("sinq", [P, 2, HEADS, 2, DH // 2])
        ss = sb("ss", [P, 2 * HEADS])
        half_ss = sb("half_ss", [P, 2 * HEADS])
        three_halves = sb("three_halves", [P, 2 * HEADS])
        ry = sb("ry", [P, 2 * HEADS])
        rt = sb("rt", [P, 2 * HEADS])
        rs = sb("rs", [P, 2 * HEADS])
        qT = sb("qT", [P, QCH, P])
        kT = [sb(f"kT{i}", [P, QCH, 2, WIN + P]) for i in range(2)]
        va = sb("va", [P, VTILES, 2, HEADS, VA])
        vb = sb("vb", [P, VTILES, 2, HEADS, VA])
        prob = sb("prob", [P, HEADS, DH])
        probT = sb("probT", [P, 8, P])
        smax = sb("smax", [P, HEADS])
        rden = sb("rden", [P, 2, 2, 4])
        o = sb("o", [P, 2, 4, 2, DH])
        oT = sb("oT", [P, QCH, SEQ])
        x1 = sb("x1", [P, SEQ])
        xs2 = sb("xs2", [P, SEQ])
        z = xs2
        xc = sb("xc", [P, SEQ])
        sqc = sb("sqc", [P, SEQ])
        gate = sqc[0:JW, :]
        hid = sb("hid", [JW, NJ, SEQ])
        slots = [ctx.enter_context(nc.psum_tensor(f"slot{i}", [P, 2, SEQ], F32)) for i in range(len(SLOTS_OF))]
        S = {n: sem("ws_" + n) for n in list(EVENTS) + ["const_loaded", "const_ready", "w_q", "w_k", "w_v", "qks_loaded", "w_ff", "tables",
                                                        "cleared", "xs_ready", "norms_link", "s_link", "va_link", "vb_link", "ff_link", "pool_link", "passed"]}
        vb_ready = [sem(f"ws_vb_ready{t}") for t in range(TPB)]
        VB_DMAS = [3] + [4] * (TPB - 1)
        W_FF = 5
        CONSTS = 6
        block = ctx.enter_context(nc.Block())

        wait = event_wait(S, EVENTS)

        def passed(eng):
            eng.sem_inc(S["passed"], 1)

        def wait_tile(eng, name, unit, t, back=1):
            wait(eng, name, unit + (t - back) // TPB, (t - back) % TPB)

        def wait_vb(eng, unit, t):
            eng.wait_ge(vb_ready[t], 16 * VB_DMAS[t] * (unit + 2))

        def slot(kind, n=0):
            return slots[SLOT[kind, n]]

        def flat(kind, n=0):
            return slot(kind, n)[:, :, :].rearrange("p a n -> p (a n)")

        def units(eng, order, stage, layer_start=None, layer_end=None):
            def step(it, l, b, first, looped):
                starts = l if isinstance(b, int) and b == 0 else None
                if starts is not None and layer_start:
                    layer_start(it, l)
                for at, (kind, n, back) in enumerate(order):
                    if looped or 0 <= first - back < DEPTH * BATCH:
                        batch = b if back == 0 else (BATCH - 1 if starts is not None else b - 1)
                        before = []
                        if order is PE_ORDER:
                            before = [(k, m, it - ago) for k, m, ago in
                                      forerunners(order, SLOT, at, first, looped, DEPTH * BATCH)]
                        stage(kind, n, it - back, batch, before, starts)
                if starts is not None and layer_end:
                    layer_end(it, l)
            step(0, 0, 0, 0, False)
            with eng.Fori(1, BATCH) as b:
                step(b, 0, b, 1, True)
            with eng.Fori(1, DEPTH) as l:
                step(l * BATCH, l, 0, BATCH, True)
                with eng.Fori(1, BATCH) as b:
                    step(l * BATCH + b, l, b, BATCH + 1, True)
            step(DEPTH * BATCH, None, BATCH, DEPTH * BATCH, False)

        @block.sync
        def _(sp):
            for t in range(TPB):
                sp.sem_inc(vb_ready[t], 16 * VB_DMAS[t])
            sp.dma_start(mask32, io["mask"]).then_inc(S["const_loaded"], 16)

            def load_ff(l):
                sp.dma_start(w_o[:, :, :], io["w_o"][l].rearrange("(c p) n -> p c n", p=P)).then_inc(S["w_ff"], 16)
                sp.dma_start(w_1[:, :, :, :].rearrange("p a j n -> p (a j n)"), io["w_1"][l]).then_inc(S["w_ff"], 16)
                sp.dma_start(w_2[:, :, :], io["w_2"][l].rearrange("(j p) n -> p j n", p=JW)).then_inc(S["w_ff"], 16)
                sp.dma_start(b_1[:, :, :].rearrange("p a j -> p (a j)"), io["b_1"][l]).then_inc(S["w_ff"], 16)
                sp.dma_start(vec[:, :], io["vec"][l]).then_inc(S["w_ff"], 16)

            def layer_start(it, l):
                for i, kind in enumerate("qkv"):
                    wait(sp, kind + "_filled", it - 1, TPB - 1)
                    passed(sp)
                    sp.dma_start(w_qkv[:, i, :], io["w_qkv"][l][:, i * INNER:(i + 1) * INNER]).then_inc(S["w_" + kind], 16)
                    if i == 0:
                        if isinstance(l, int):
                            sp.dma_start(rot[:, :, :, :], io["rot"]).then_inc(S["const_loaded"], 16)
                        sp.dma_start(qks[:, :, :].rearrange("p a n -> p (a n)"), io["qk_scale"][l]).then_inc(S["qks_loaded"], 16)
                if isinstance(l, int):
                    load_ff(0)

            def layer_end(it, l):
                if not isinstance(l, int):
                    wait(sp, "y_read", it - 1)
                    load_ff(l)

            def stage(kind, t, unit, batch, before, starts):
                s = t % VTILES
                wait(sp, "v_read", unit, t)
                sp.dma_start(vb[32:64, s, 0, :, :], va[0:32, s, 0, :, :]).then_inc(vb_ready[t], 16)
                sp.dma_start(vb[64:96, s, 1, :, :], va[32:64, s, 0, :, :]).then_inc(vb_ready[t], 16)
                sp.dma_start(vb[96:128, s, 1, :, :], va[64:96, s, 1, :, :]).then_inc(vb_ready[t], 16)
                if t:
                    sp.dma_start(vb[0:32, s, 0, :, :], va[96:128, (t - 1) % VTILES, 1, :, :]).then_inc(vb_ready[t], 16)
            units(sp, SP_ORDER, stage, layer_start, layer_end)

        @block.gpsimd
        def _(pool):
            credit(pool, S, EVENTS, "pool")
            for k in kT:
                pool.memset(k[:, :, :, :], 0.0).then_inc(S["cleared"], 1)
            for buffer, value in ((ones, 1.0 / D), (zero, 0.0), (epsc, EPS), (three_halves, 1.5), (xs, 0.0), (xs2, 0.0)):
                pool.memset(buffer[:, :], value).then_inc(S["cleared"], 1)
            pool.wait_ge(S["cleared"], 10)
            for v in (va, vb):
                pool.memset(v[0:DH, :, 0, :, DH:VA], 1.0).then_inc(S["const_ready"], 1)
                pool.memset(v[DH:P, :, 1, :, DH:VA], 1.0).then_inc(S["const_ready"], 1)
            STEPS = 3
            LINKS = 4 * STEPS - 1

            def stage(kind, t, unit, batch, before, starts):
                if kind == "root":
                    wait(pool, "seeded", unit, t)
                    for k in range(STEPS):
                        for i, (dst, a, b, op) in enumerate(((rt, ry, ry, ALU.mult), (rt, rt, half_ss, ALU.mult),
                                                             (rt, rt, three_halves, ALU.add), (ry, ry, rt, ALU.mult))):
                            last = nc.gpsimd.tensor_tensor(dst[:, :], a[:, :], b[:, :], op)
                            if 4 * k + i < LINKS:
                                last.then_inc(S["pool_link"], 1)
                                pool.wait_ge(S["pool_link"], (unit * TPB + t) * LINKS + 4 * k + i + 1)
                    last.then_inc(S["rooted"], 1)
                else:
                    side = ("add_q", "add_k").index(kind)
                    wait(pool, "qk"[side] + "_read", unit, t)
                    nc.gpsimd.tensor_tensor(cosq[:, side], cosq[:, side], sinq[:, side], ALU.add).then_inc(
                        S["qk"[side] + "_added"], 1)
            units(pool, POOL_ORDER, stage)

        @block.vector
        def _(dve):
            credit(dve, S, EVENTS, "dve")
            for v in (va, vb):
                nc.vector.memset(v[:, :, :, :, :], 0.0).then_inc(S["cleared"], 1)
            dve.wait_ge(S["const_loaded"], 32)
            nc.vector.tensor_copy(mask[:, :, :], mask32).then_inc(S["const_ready"], 1)
            nc.vector.tensor_copy(ident16[:, :], ident[:, :]).then_inc(S["const_ready"], 1)
            dve.wait_ge(S["const_ready"], CONSTS)
            H = DH // 2
            LINKS = {"norms": 2, "s": 1, "va": 1, "vb": 1}

            def layer_tables(it, l):
                for name in "qk":
                    wait(dve, name + "_read", it - 1, TPB - 1)
                dve.wait_ge(S["qks_loaded"], 16 * (l + 1))
                for side in range(2):
                    s = qks[:, side, :]
                    nc.vector.tensor_tensor(table[:, :, 2 * side, :], rot[:, :, 2 * side, :],
                                            s[:, None, :].broadcast_to([P, TPB, DH]), ALU.mult)
                    for half in range(2):
                        other = s[:, (1 - half) * H:(2 - half) * H]
                        last = nc.vector.tensor_tensor(
                            table[:, :, 2 * side + 1, half * H:half * H + H], rot[:, :, 2 * side + 1, half * H:half * H + H],
                            other[:, None, :].broadcast_to([P, TPB, H]), ALU.mult)
                last.then_inc(S["tables"], 1)
                dve.wait_ge(S["tables"], l + 1)
                passed(dve)

            def layer_end(it, l):
                dve.wait_ge(S["w_ff"], 16 * W_FF * (l + 1))
                passed(dve)

            def rotate(side, t, unit):
                name = "qk"[side]
                ps = flat(name, t).rearrange("p (h a d) -> p h a d", h=HEADS, a=2)
                cos, sin = table[:, t, 2 * side, :], table[:, t, 2 * side + 1, :]
                wait(dve, name + "_squared", unit, t)
                wait_tile(dve, name + "_scaled", unit, t)
                nc.vector.tensor_tensor(cosq[:, side].rearrange("p h a d -> p h (a d)"), ps.rearrange("p h a d -> p h (a d)"),
                                        cos[:, None, :].broadcast_to([P, HEADS, DH]), ALU.mult)
                for half in range(2):
                    last = nc.vector.tensor_tensor(
                        sinq[:, side, :, half, :], ps[:, :, 1 - half, :],
                        sin[:, None, half * H:half * H + H].broadcast_to([P, HEADS, H]), ALU.mult)
                last.then_inc(S[name + "_read"], 1)

            def stage(kind, n, unit, batch, before, starts):
                def link(ins, name, i):
                    ins.then_inc(S[name + "_link"], 1)
                    dve.wait_ge(S[name + "_link"], (unit * TPB + n) * LINKS[name] + i + 1)

                if (kind, n) == ROTATIONS[0] and starts is not None:
                    layer_tables(unit, starts)
                if kind in ("rotate_q", "rotate_k"):
                    rotate(("rotate_q", "rotate_k").index(kind), n, unit)
                elif kind == "norms":
                    for name in "qk":
                        wait(dve, name + "_squared", unit, n)
                        wait_tile(dve, name + "_scaled", unit, n)
                    nc.vector.reduce_sum(ss[:, :], sq[:, :, :, :].rearrange("p a h d -> p (a h) d"), AX.X).then_inc(S["sumsq"], 1)
                    wait(dve, "sumsq", unit, n)
                    link(nc.vector.tensor_scalar(ss[:, :], ss[:, :], 1e-24, None, ALU.max), "norms", 0)
                    nc.vector.tensor_scalar(half_ss[:, :], ss[:, :], -0.5, None, ALU.mult)
                    link(nc.vector.tensor_single_scalar(rs[:, :].bitcast(I32), ss[:, :].bitcast(I32), 1, ALU.logical_shift_right),
                         "norms", 1)
                    nc.vector.tensor_scalar(ry[:, :].bitcast(I32), rs[:, :].bitcast(I32), -1.0, float(0x5F3759DF),
                                            ALU.mult, ALU.add).then_inc(S["seeded"], 1)
                elif kind in ("scale_q", "scale_k"):
                    side = ("scale_q", "scale_k").index(kind)
                    name = "qk"[side]
                    wait(dve, name + "_added", unit, n)
                    wait(dve, "rooted", unit, n)
                    wait_tile(dve, name + "T_filled", unit, n)
                    nc.vector.tensor_tensor(qk[:, side], cosq[:, side].rearrange("p h a d -> p h (a d)"),
                                            ry[:, side * HEADS:(side + 1) * HEADS, None].broadcast_to([P, HEADS, DH]),
                                            ALU.mult).then_inc(S[name + "_scaled"], 1)
                elif kind == "s":
                    wait(dve, "s_filled", unit, n)
                    wait_tile(dve, "r_filled", unit, n)
                    ps = flat("s", n).rearrange("p (s k) -> p s k", k=DH)
                    link(nc.vector.reduce_max(smax[:, :], ps, AX.X), "s", 0)
                    nc.vector.tensor_tensor(prob[:, :, :], ps, smax[:, :, None].broadcast_to([P, HEADS, DH]),
                                            ALU.subtract).then_inc(S["s_read"], 1)
                elif kind in ("va", "vb"):
                    a = ("va", "vb").index(kind)
                    wait(dve, kind + "_filled", unit, n)
                    wait_tile(dve, "o_filled", unit, n)
                    ps = slot(kind, n)[:, :, 0:4 * VA].rearrange("p r (w d) -> p r w d", d=VA)
                    link(nc.vector.reciprocal(rden[:, a], ps[:, :, :, DH]), kind, 0)
                    nc.vector.tensor_tensor(o[:, a].rearrange("p w r d -> p r w d"), ps[:, :, :, 0:DH],
                                            rden[:, a, :, :, None].broadcast_to([P, 2, 4, DH]), ALU.mult).then_inc(S[kind + "_read"], 1)
                elif kind == "residual":
                    wait(dve, "wo_filled", unit)
                    wait(dve, "y_read", unit - 1)
                    nc.vector.tensor_tensor(x1[:, :], slot("wo")[:, 0, :], xT[:, batch, :], ALU.add).then_inc(S["wo_read"], 1)
                elif kind == "center":
                    wait(dve, "mean_filled", unit)
                    nc.vector.tensor_tensor(xc[:, :], xs2[:, :], slot("mean")[:, 0, :], ALU.subtract).then_inc(S["mean_read"], 1)
                elif kind == "z":
                    wait(dve, "var_read", unit)
                    nc.vector.reciprocal(sqc[:, :], sqc[:, :]).then_inc(S["ff_link"], 1)
                    dve.wait_ge(S["ff_link"], 2 * unit + 1)
                    nc.vector.tensor_tensor(z[:, :], xc[:, :], sqc[:, :], ALU.mult).then_inc(S["ff_link"], 1)
                    dve.wait_ge(S["ff_link"], 2 * unit + 2)
                    nc.vector.tensor_scalar(z[:, :], z[:, :], vec[:, 0:1], vec[:, 1:2], ALU.mult, ALU.add).then_inc(S["z_ready"], 1)
                elif kind == "hid":
                    wait(dve, "gates", unit, n)
                    nc.vector.scalar_tensor_tensor(out=hid[:, n, :], in0=slot("h", n)[0:JW, 0, :], scalar=b_1[:, 0, n:n + 1],
                                                   in1=gate, op0=ALU.add, op1=ALU.mult).then_inc(S["h_read"], 1)
                elif kind == "y":
                    wait(dve, "y_filled", unit)
                    nc.vector.scalar_tensor_tensor(out=xT[:, batch, :], in0=slot("y")[:, 0, :], scalar=vec[:, 2:3],
                                                   in1=x1[:, :], op0=ALU.add, op1=ALU.add).then_inc(S["y_read"], 1)
            units(dve, DVE_ORDER, stage, None, layer_end)

        @block.scalar
        def _(act):
            credit(act, S, EVENTS, "act")
            act.wait_ge(S["const_ready"], CONSTS)

            def shift_tokens(dst, src, done):
                nc.scalar.copy(dst[0:DH, :], src[0:DH])
                nc.scalar.copy(dst[DH:P, 1:SEQ], src[DH:P, 0:SEQ - 1]).then_inc(done, 1)

            def layer_end(it, l):
                act.wait_ge(S["w_ff"], 16 * W_FF * (l + 1))
                passed(act)

            def stage(kind, n, unit, batch, before, starts):
                if kind in ("square_q", "square_k"):
                    name = kind[-1]
                    wait(act, name + "_filled", unit, n)
                    wait_tile(act, "sumsq", unit, n)
                    nc.scalar.activation(sq[:, "qk".index(name)].rearrange("p h d -> p (h d)"), flat(name, n),
                                         ACT.Square).then_inc(S[name + "_squared"], 1)
                elif kind == "v":
                    old, unit_of = (0, unit) if n == VTILES else ((TPB - 1 if n == 0 else n), unit - 1)
                    wait(act, "vb_filled", unit_of, old)
                    wait_vb(act, unit_of, old)
                    if old + 1 < TPB:
                        wait_vb(act, unit_of, old + 1)
                    wait(act, "v_filled", unit, n)
                    ps = flat("v", n).rearrange("p (h d) -> p h d", d=DH)
                    nc.scalar.copy(va[0:DH, n % VTILES, 0, :, 0:DH], ps[0:DH])
                    nc.scalar.copy(va[DH:P, n % VTILES, 1, :, 0:DH], ps[DH:P]).then_inc(S["v_read"], 1)
                elif kind == "qT":
                    wait(act, "qT_filled", unit, n)
                    wait_tile(act, "s_filled", unit, n)
                    nc.scalar.copy(qT[:, :, :], flat("qT", n).rearrange("p (c n) -> p c n", n=P)).then_inc(S["qT_read"], 1)
                elif kind == "kT":
                    wait(act, "kT_filled", unit, n)
                    wait_tile(act, "s_filled", unit, n)
                    ps = flat("kT", n).rearrange("p (c n) -> p c n", n=P)
                    own, following = kT[n % 2], kT[(n + 1) % 2]
                    for r, rows in enumerate((slice(0, DH), slice(DH, P))):
                        nc.scalar.copy(own[rows, :, r, WIN:WIN + P], ps[rows])
                        last = nc.scalar.copy(following[rows, :, r, 0:WIN], ps[rows, :, P - WIN:P])
                    last.then_inc(S["kT_read"], 1)
                elif kind == "exp":
                    wait(act, "s_read", unit, n)
                    nc.scalar.activation(prob[:, :, :], prob[:, :, :], ACT.Exp).then_inc(S["probs"], 1)
                elif kind == "r":
                    wait(act, "r_filled", unit, n)
                    wait_tile(act, "vb_filled", unit, n)
                    nc.scalar.copy(probT[:, :, :], flat("r", n).rearrange("p (c n) -> p c n", n=P)).then_inc(S["r_read"], 1)
                elif kind == "o":
                    wait(act, "o_filled", unit, n)
                    wait(act, "wo_filled", unit - 1)
                    nc.scalar.copy(oT[:, :, n * P:(n + 1) * P].rearrange("p c (w n) -> p w c n", n=WIN),
                                   flat("o", n).rearrange("p (w c n) -> p w c n", w=4, n=WIN)).then_inc(S["o_read"], 1)
                elif kind == "next":
                    last_kind, last_n = PROJECTIONS[-1]
                    wait(act, last_kind + "_filled", unit, last_n)
                    shift_tokens(xs, xT[:, batch + 1 if isinstance(batch, int) else (batch + 1) % BATCH, :], S["xs_ready"])
                elif kind == "shift":
                    wait(act, "wo_read", unit)
                    wait(act, "h_filled", unit - 1, NJ - 1)
                    nc.scalar.mul(xs2[DH:P, 0:1], zero[DH:P, 0:1], 0.0)
                    shift_tokens(xs2, x1, S["xs2_ready"])
                elif kind == "square":
                    wait(act, "mean_read", unit)
                    nc.scalar.activation(sqc[:, :], xc[:, :], ACT.Square).then_inc(S["centered_sq"], 1)
                elif kind == "root":
                    wait(act, "var_filled", unit)
                    nc.scalar.activation(sqc[:, :], slot("var")[:, 0, :], ACT.Sqrt, bias=epsc[:, 0:1]).then_inc(S["var_read"], 1)
                elif kind == "gate":
                    if n:
                        wait(act, "h_read", unit, n - 1)
                    wait(act, "h_filled", unit, n)
                    nc.scalar.activation(gate, slot("h", n)[0:JW, 1, :], ACT.Gelu, bias=b_1[:, 1, n:n + 1]).then_inc(S["gates"], 1)
            shift_tokens(xs, xT[:, 0, :], S["xs_ready"])
            units(act, ACT_ORDER, stage, None, layer_end)

        @block.tensor
        def _(pe):
            credit(pe, S, EVENTS, "pe")
            pe.wait_ge(S["const_ready"], CONSTS)

            def layer_end(it, l):
                pe.wait_ge(S["w_ff"], 16 * W_FF * (l + 1))
                passed(pe)

            def transposes(kind, n, src, place=lambda c: c):
                for c in range(8):
                    k = place(c)
                    last = nc.tensor.transpose(flat(kind, n)[:, k * P:(k + 1) * P], src[:, c * P:(c + 1) * P], ident[:, :])
                return last

            def scores(t):
                for a in range(2):
                    nc.tensor.matmul(slot("s", t)[:, a, :], ident16[:, :], mask[:, 0 if t == 0 else 1, :],
                                     start=True, stop=False, skip_group_check=True)
                    for n, w in enumerate(WINDOWS):
                        tok = WIN * w
                        for g in range(4):
                            c = 4 * a + g
                            last = nc.tensor.matmul(
                                slot("s", t)[32 * g:32 * g + 32, a, :].rearrange("p (r k) -> p r k", r=2)[
                                    :, :, n * DH:(n + 1) * DH],
                                qT[:, c, tok:tok + WIN], kT[t % 2][:, c, :, tok:tok + 2 * WIN],
                                start=False, stop=True, skip_group_check=True)
                return last

            def products(kind, t):
                a = ("va", "vb").index(kind)
                for r in range(2):
                    for n, v in enumerate((va, vb)):
                        for g in range(4):
                            last = nc.tensor.matmul(
                                slot(kind, t)[32 * g:32 * g + 32, r, 2 * n * VA:2 * (n + 1) * VA],
                                probT[:, 4 * a + 2 * r + n, 32 * g:32 * g + 32],
                                v[:, t % VTILES, :, 2 * (4 * a + g) + r, :],
                                start=True, stop=True, skip_group_check=True)
                return last

            def stage(kind, n, unit, batch, before, starts):
                for filled, m, of in before:
                    wait(pe, filled + "_read", of, m)
                if kind in ("q", "k", "v"):
                    if (kind, n) == PROJECTIONS[0]:
                        pe.wait_ge(S["xs_ready"], unit + 1)
                    if n == 0 and starts is not None:
                        pe.wait_ge(S["w_" + kind], 16 * (starts + 1))
                        passed(pe)
                    for i in range(2):
                        last = nc.tensor.matmul(slot(kind, n)[:, i, :], xs[:, n * P:(n + 1) * P],
                                                w_qkv[:, "qkv".index(kind), i * SEQ:(i + 1) * SEQ], start=True, stop=True)
                elif kind in ("qT", "kT"):
                    wait(pe, kind[0] + "_scaled", unit, n)
                    last = transposes(kind, n, qk[:, "qk".index(kind[0])].rearrange("p h d -> p (h d)"))
                elif kind == "s":
                    wait(pe, "qT_read", unit, n)
                    wait(pe, "kT_read", unit, n)
                    last = scores(n)
                elif kind == "r":
                    wait(pe, "probs", unit, n)
                    last = transposes(kind, n, prob[:, :, :].rearrange("p h d -> p (h d)"))
                elif kind in ("va", "vb"):
                    if kind == "va":
                        wait(pe, "r_read", unit, n)
                        wait_vb(pe, unit, n)
                    passed(pe)
                    last = products(kind, n)
                elif kind == "o":
                    wait(pe, "va_read", unit, n)
                    wait(pe, "vb_read", unit, n)
                    last = transposes(kind, n, o[:, :, :, :, :].rearrange("p a w r d -> p (a w r d)"),
                                      lambda c: 2 * WINDOWS[c % 4] + c // 4)
                elif kind == "wo":
                    wait(pe, "o_read", unit, TPB - 1)
                    for c in range(QCH):
                        last = nc.tensor.matmul(slot("wo")[:, 0, :], w_o[:, c, :], oT[:, c, :], start=c == 0, stop=c == QCH - 1)
                elif kind == "mean":
                    wait(pe, "xs2_ready", unit)
                    last = nc.tensor.matmul(slot("mean")[:, 0, :], ones[:, :], xs2[:, :], start=True, stop=True)
                elif kind == "var":
                    wait(pe, "centered_sq", unit)
                    last = nc.tensor.matmul(slot("var")[:, 0, :], ones[:, :], sqc[:, :], start=True, stop=True)
                elif kind == "h":
                    wait(pe, "z_ready", unit)
                    for a in (1, 0):
                        last = nc.tensor.matmul(slot("h", n)[0:JW, a, :], w_1[:, a, n, :], z[:, :], start=True, stop=True)
                elif kind == "y":
                    wait(pe, "h_read", unit, NJ - 1)
                    for j in range(NJ):
                        last = nc.tensor.matmul(slot("y")[:, 0, :], w_2[:, j, :], hid[:, j, :], start=j == 0, stop=j == NJ - 1)
                last.then_inc(S[kind + "_filled"], 1)
            units(pe, PE_ORDER, stage, None, layer_end)


def add_up(nc, io, xT, ident):
    with ExitStack() as ctx:
        res = ctx.enter_context(nc.sbuf_tensor("fin_res", [P, TILES, D], F32))
        fetched = ctx.enter_context(nc.semaphore("fin_fetched"))
        sem = lambda n: ctx.enter_context(nc.semaphore(n))
        ps = [ctx.enter_context(nc.psum_tensor(f"fin_ps{i}", [P, 4 * P], F32)) for i in range(2)]
        turned, summed, stored = sem("fin_turned"), sem("fin_summed"), sem("fin_stored")
        block = ctx.enter_context(nc.Block())

        @block.tensor
        def _(pe):
            for b in range(BATCH):
                if b >= 2:
                    pe.wait_ge(summed, b - 1)
                for t in range(TPB):
                    last = nc.tensor.transpose(ps[b % 2][:, t * P:(t + 1) * P], xT[:, b, t * P:(t + 1) * P], ident[:, :])
                last.then_inc(turned, 1)

        @block.vector
        def _(dve):
            dve.wait_ge(fetched, 16)
            for b in range(BATCH):
                dve.wait_ge(turned, b + 1)
                r = res[:, TPB * b:TPB * (b + 1), :]
                nc.vector.tensor_tensor(r, r, ps[b % 2][:, :].rearrange("p (t d) -> p t d", d=D), ALU.add).then_inc(summed, 1)

        @block.sync
        def _(sp):
            sp.dma_start(res[:, :, :], io["kept"].rearrange("(n p) d -> p n d", p=P)).then_inc(fetched, 16)
            out = io["out"].rearrange("(n p) d -> p n d", p=P)
            for b in range(BATCH):
                sp.wait_ge(summed, b + 1)
                sp.dma_start(out[:, TPB * b:TPB * (b + 1), :], res[:, TPB * b:TPB * (b + 1), :]).then_inc(stored, 16)
            sp.wait_ge(stored, 16 * BATCH)


def build(nc, io):
    with nc.sbuf_tensor("xT", [P, BATCH, SEQ], F32) as xT, nc.sbuf_tensor("ident", [P, P], F32) as ident:
        with nc.sbuf_tensor("res", [P, TILES, D], F32) as res:
            layer_norm_and_transpose(nc, io, res, xT, ident)
            global_attention(nc, io, res, xT, ident)
        windowed_stack(nc, io, xT, ident)
        add_up(nc, io, xT, ident)


def rotation_tables():
    half = np.arange(0, DH, 2, dtype=np.float64)
    t = np.arange(SEQ, dtype=np.float64)
    freqs = t[:, None] * (1.0 / 10000.0 ** (half / DH))[None, :]
    scale = ((half + 0.4 * DH) / (1.4 * DH))[None, :] ** ((t - SEQ // 2) / (WIN // 2))[:, None]
    sign = np.concatenate([-np.ones(DH // 2), np.ones(DH // 2)])
    two = lambda a: np.concatenate([a, a], -1)
    cos, sin, scale = two(np.cos(freqs)), two(np.sin(freqs)) * sign, two(scale)
    kinds = np.stack([8.0 * cos * scale, 8.0 * sin * scale, cos / scale, sin / scale], 1)
    return np.ascontiguousarray(kinds.reshape(TPB, P, 4, DH).transpose(1, 0, 2, 3).astype(np.float32))


def window_masks():
    i = np.arange(P)[:, None] % WIN
    j = np.arange(2 * WIN)[None, :]
    block = np.where((j >= i) & (j <= i + WIN), 0.0, MASKED)
    first = np.where((j >= WIN) & (j <= i + WIN), 0.0, MASKED)
    rows = lambda w0: np.tile(np.concatenate([block, block, w0, block], 1), (1, 2))
    return np.ascontiguousarray(np.stack([rows(first), rows(block)], 1).astype(np.float32))


def kernel(**inputs):
    import concourse.bacc as bacc
    from concourse.bass_utils import run_bass_kernel_spmd

    f = {k[3:]: np.asarray(v) for k, v in inputs.items()}
    w = f["attn_Wqkv"].reshape(CH, 3, HD, D).transpose(3, 1, 0, 2).reshape(D, 3 * D)
    bq = f["attn_bqkv"].reshape(CH, 3, HD).transpose(1, 0, 2).reshape(1, 3 * D)
    w1 = np.zeros((DEPTH, D, 2, NJ * JW), np.float32)
    w1[:, :, :, :DIN] = f["ffn_W1"].reshape(DEPTH, D, 2, DIN)
    b1 = np.zeros((DEPTH, 2, NJ * JW), np.float32)
    b1[:, :, :DIN] = f["ffn_b1"].reshape(DEPTH, 2, DIN)
    w2 = np.zeros((DEPTH, NJ * JW, D), np.float32)
    w2[:, :DIN] = f["ffn_W2"]
    scales = np.concatenate([f["ffn_q_scale"], f["ffn_k_scale"]], 1)[:, None, :]
    arrays = {
        "x": f["attn_x"].reshape(TOKENS, D),
        "ident": np.eye(P, dtype=np.float32),
        "bo_rows": np.broadcast_to(f["attn_bo"], (P, D)),
        "at_wqkvT": w,
        "at_woT": f["attn_Wo"].T,
        "at_bias": np.broadcast_to(bq, (P, 3 * D)),
        "rot": rotation_tables(),
        "mask": window_masks(),
        "w_qkv": f["ffn_Wqkv"],
        "qk_scale": np.broadcast_to(scales, (DEPTH, P, 2 * DH)),
        "w_o": f["ffn_Wo"],
        "w_1": w1.reshape(DEPTH, D, 2 * NJ * JW),
        "w_2": w2,
        "b_1": b1.reshape(DEPTH, 2, NJ, JW).transpose(0, 3, 1, 2).reshape(DEPTH, JW, 2 * NJ),
        "vec": np.stack([f["ffn_ln_g"], f["ffn_ln_b"], f["ffn_b2"]], 2),
    }
    arrays = {f"in_{k}": np.ascontiguousarray(v) for k, v in arrays.items()}
    nc = bacc.Bacc("TRN2", target_bir_lowering=False, num_devices=1)
    io = {k[3:]: nc.dram_tensor(k, v.shape, F32, kind="ExternalInput").ap() for k, v in arrays.items()}
    io["out"] = nc.dram_tensor("out_0", (TOKENS, D), F32, kind="ExternalOutput").ap()
    io["kept"] = nc.dram_tensor("kept", (TOKENS, D), F32, kind="Internal").ap()
    build(nc, io)
    r = run_bass_kernel_spmd(nc, [arrays], core_ids=[0])
    return r.results[0]["out_0"].reshape(BATCH, SEQ, D)
```
